# Optimizing a Trainium2 kernel written in Bass

```python
import numpy as np
import jax
import jax.numpy as jnp

def _softmax(x, axis=-1):
    return jax.nn.softmax(x, axis=axis)

def _gelu(x):
    return jax.nn.gelu(x, approximate=True)

def _silu(x):
    return jax.nn.silu(x)

def _sigmoid(x):
    return jax.nn.sigmoid(x)

def _layernorm(x, axis=-1, eps=1e-05):
    m = jnp.mean(x, axis=axis, keepdims=True)
    v = jnp.var(x, axis=axis, keepdims=True)
    return (x - m) / jnp.sqrt(v + eps)

def _scatter_add(tgt, idx, src, axis=0):
    return tgt.at[idx].add(src)

def _segment_sum(src, seg, n):
    return jax.ops.segment_sum(src, seg, n)
kernel_name = 'mk_conv_preact_d2_conv_nhwc256_r4_dc814e'

def setup_inputs(seed: int=0):
    np.random.seed(seed)
    _w = jnp.asarray

    def _rec_inputs():
        import jax
        import jax.numpy as jnp
        _gk = jax.random.key(seed)
        x = 7.22e-05 + 1 * jax.random.normal(jax.random.fold_in(_gk, 1), (32, 32, 32, 64), jnp.float32)
        return x
    x = _rec_inputs()

    def _L0_conv_setup():
        import jax, jax.numpy as jnp
        import numpy as np
        K = 4
        STEPS = 3
        TOP_N = 2
        HEADS = 2
        DIM_HEAD = 16
        ROUTE_TEMP = 1.5
        C = 64

        def conv3x3(x, w, b):
            y = jax.lax.conv_general_dilated(x, w, window_strides=(1, 1), padding='SAME', dimension_numbers=('NHWC', 'HWIO', 'NHWC'))
            return y + b
        key = jax.random.key(seed)
        ks = jax.random.split(key, 8)
        B, H, W = (32, 32, 32)
        D = HEADS * DIM_HEAD
        glorot = jax.nn.initializers.glorot_uniform()
        x = jax.random.normal(ks[0], (B, H, W, C), dtype=jnp.float32)
        q = glorot(ks[1], (HEADS, DIM_HEAD), jnp.float32)
        Wk = glorot(ks[2], (C, D), jnp.float32)
        Wv = glorot(ks[3], (C, D), jnp.float32)
        Wmlp = glorot(ks[4], (D, K), jnp.float32)
        alpha = jnp.zeros((), jnp.float32)
        We = glorot(ks[5], (K * 3, 3, C, C), jnp.float32).reshape(K, 3, 3, C, C)
        be = jnp.zeros((K, C), jnp.float32)
        return {'x': x, 'q': q, 'Wk': Wk, 'Wv': Wv, 'Wmlp': Wmlp, 'alpha': alpha, 'We': We, 'be': be}
    _L0_conv_all = _L0_conv_setup()
    _L0_conv_in = {k: v for k, v in _L0_conv_all.items() if k in ('q', 'Wk', 'Wv', 'Wmlp', 'alpha', 'We', 'be')}
    del _L0_conv_all

    def _L1_conv_setup():
        import jax, jax.numpy as jnp
        from jax import lax
        import numpy as np
        D_MODEL, D_STATE, D_CONV, EXPAND = (64, 16, 4, 2)
        D_INNER = EXPAND * D_MODEL
        DT_RANK = (D_MODEL + 15) // 16
        B, NVAR, SEG = (4, 32, 24)

        def _mamba_params(key, scale=0.02):
            ks = jax.random.split(key, 7)
            in_w = jax.random.normal(ks[0], (2 * D_INNER, D_MODEL)) * scale
            conv_w = jax.random.normal(ks[1], (D_INNER, D_CONV)) * scale
            conv_b = jnp.zeros((D_INNER,))
            xproj_w = jax.random.normal(ks[2], (DT_RANK + 2 * D_STATE, D_INNER)) * scale
            dt_w = jax.random.normal(ks[3], (D_INNER, DT_RANK)) * scale
            dt = jnp.exp(jax.random.uniform(ks[4], (D_INNER,)) * (np.log(0.1) - np.log(0.001)) + np.log(0.001))
            dt_b = dt + jnp.log(-jnp.expm1(-dt))
            A_log = jnp.log(jnp.broadcast_to(jnp.arange(1, D_STATE + 1, dtype=jnp.float32), (D_INNER, D_STATE)))
            Dvec = jnp.ones((D_INNER,))
            out_w = jax.random.normal(ks[5], (D_MODEL, D_INNER)) * scale
            return (in_w, conv_w, conv_b, xproj_w, dt_w, dt_b, A_log, Dvec, out_w)

        def _mamba(x, in_w, conv_w, conv_b, xproj_w, dt_w, dt_b, A_log, Dvec, out_w):
            Bn, L, _ = x.shape
            xz = jnp.einsum('bld,ed->ble', x, in_w)
            xi, z = jnp.split(xz, 2, axis=-1)
            xi_nc = xi.transpose(0, 2, 1)
            xc = lax.conv_general_dilated(xi_nc, conv_w[:, None, :], (1,), [(D_CONV - 1, 0)], feature_group_count=D_INNER)
            xc = jax.nn.silu(xc + conv_b[None, :, None]).transpose(0, 2, 1)
            dbl = jnp.einsum('ble,fe->blf', xc, xproj_w)
            dt, Bm, Cm = jnp.split(dbl, [DT_RANK, DT_RANK + D_STATE], axis=-1)
            dt = jax.nn.softplus(jnp.einsum('blr,er->ble', dt, dt_w) + dt_b)
            A = -jnp.exp(A_log)

            def step(h, inp):
                dt_t, B_t, C_t, u_t = inp
                dA = jnp.exp(dt_t[:, :, None] * A)
                h = dA * h + dt_t[:, :, None] * B_t[:, None, :] * u_t[:, :, None]
                y = jnp.einsum('bes,bs->be', h, C_t)
                return (h, y)
            h0 = jnp.zeros((Bn, D_INNER, D_STATE), x.dtype)
            _, ys = lax.scan(step, h0, (dt.transpose(1, 0, 2), Bm.transpose(1, 0, 2), Cm.transpose(1, 0, 2), xc.transpose(1, 0, 2)))
            y = ys.transpose(1, 0, 2) + xc * Dvec
            y = y * jax.nn.silu(z)
            return jnp.einsum('ble,de->bld', y, out_w)
        key = jax.random.key(seed)
        kx, kt, kd = jax.random.split(key, 3)
        x = jax.random.normal(kx, (B, NVAR, SEG, D_MODEL), dtype=jnp.float32)
        t = _mamba_params(kt)
        d = _mamba_params(kd)
        names = ['in_w', 'conv_w', 'conv_b', 'xproj_w', 'dt_w', 'dt_b', 'A_log', 'D', 'out_w']
        inp = {'x': x}
        inp.update({f't_{n}': v for n, v in zip(names, t)})
        inp.update({f'd_{n}': v for n, v in zip(names, d)})
        return inp
    _L1_conv_all = _L1_conv_setup()
    _L1_conv_in = {k: v for k, v in _L1_conv_all.items() if k in ('t_in_w', 't_conv_w', 't_conv_b', 't_xproj_w', 't_dt_w', 't_dt_b', 't_A_log', 't_D', 't_out_w', 'd_in_w', 'd_conv_w', 'd_conv_b', 'd_xproj_w', 'd_dt_w', 'd_dt_b', 'd_A_log', 'd_D', 'd_out_w')}
    del _L1_conv_all
    return {'x': x, 'L0_conv_q': _L0_conv_in['q'], 'L0_conv_Wk': _L0_conv_in['Wk'], 'L0_conv_Wv': _L0_conv_in['Wv'], 'L0_conv_Wmlp': _L0_conv_in['Wmlp'], 'L0_conv_alpha': _L0_conv_in['alpha'], 'L0_conv_We': _L0_conv_in['We'], 'L0_conv_be': _L0_conv_in['be'], 'L1_conv_t_in_w': _L1_conv_in['t_in_w'], 'L1_conv_t_conv_w': _L1_conv_in['t_conv_w'], 'L1_conv_t_conv_b': _L1_conv_in['t_conv_b'], 'L1_conv_t_xproj_w': _L1_conv_in['t_xproj_w'], 'L1_conv_t_dt_w': _L1_conv_in['t_dt_w'], 'L1_conv_t_dt_b': _L1_conv_in['t_dt_b'], 'L1_conv_t_A_log': _L1_conv_in['t_A_log'], 'L1_conv_t_D': _L1_conv_in['t_D'], 'L1_conv_t_out_w': _L1_conv_in['t_out_w'], 'L1_conv_d_in_w': _L1_conv_in['d_in_w'], 'L1_conv_d_conv_w': _L1_conv_in['d_conv_w'], 'L1_conv_d_conv_b': _L1_conv_in['d_conv_b'], 'L1_conv_d_xproj_w': _L1_conv_in['d_xproj_w'], 'L1_conv_d_dt_w': _L1_conv_in['d_dt_w'], 'L1_conv_d_dt_b': _L1_conv_in['d_dt_b'], 'L1_conv_d_A_log': _L1_conv_in['d_A_log'], 'L1_conv_d_D': _L1_conv_in['d_D'], 'L1_conv_d_out_w': _L1_conv_in['d_out_w']}

def reference(x, L0_conv_q, L0_conv_Wk, L0_conv_Wv, L0_conv_Wmlp, L0_conv_alpha, L0_conv_We, L0_conv_be, L1_conv_t_in_w, L1_conv_t_conv_w, L1_conv_t_conv_b, L1_conv_t_xproj_w, L1_conv_t_dt_w, L1_conv_t_dt_b, L1_conv_t_A_log, L1_conv_t_D, L1_conv_t_out_w, L1_conv_d_in_w, L1_conv_d_conv_w, L1_conv_d_conv_b, L1_conv_d_xproj_w, L1_conv_d_dt_w, L1_conv_d_dt_b, L1_conv_d_A_log, L1_conv_d_D, L1_conv_d_out_w):
    import jax
    import jax.numpy as jnp

    def _L0_conv_ref(x, q, Wk, Wv, Wmlp, alpha, We, be):
        import jax, jax.numpy as jnp
        import numpy as np
        K = 4
        STEPS = 3
        TOP_N = 2
        HEADS = 2
        DIM_HEAD = 16
        ROUTE_TEMP = 1.5
        C = 64

        def conv3x3(x, w, b):
            y = jax.lax.conv_general_dilated(x, w, window_strides=(1, 1), padding='SAME', dimension_numbers=('NHWC', 'HWIO', 'NHWC'))
            return y + b
        B, H, W, Cc = x.shape
        S = H * W
        allowed = jnp.ones((B, K), x.dtype)
        last_oh = jax.nn.one_hot(jnp.full((B,), K - 1), K, dtype=x.dtype)
        scale = jnp.asarray(S, x.dtype)
        a = jax.nn.softplus(alpha)
        for t in range(STEPS):
            k = jnp.einsum('bhwc,cd->bhwd', x, Wk).reshape(B, S, HEADS, DIM_HEAD)
            v = jnp.einsum('bhwc,cd->bhwd', x, Wv).reshape(B, S, HEADS, DIM_HEAD)
            attn = jax.nn.softmax(jnp.einsum('nd,bsnd->bns', q, k) / jnp.sqrt(jnp.asarray(DIM_HEAD, x.dtype)), axis=-1)
            pooled = jnp.einsum('bns,bsnd->bnd', attn, v).reshape(B, HEADS * DIM_HEAD)
            logits = pooled @ Wmlp
            attn_map = attn.mean(axis=1).reshape(B, H, W, 1)
            masked_logits = jnp.where(allowed > 0.5, logits, jnp.asarray(-1000000000.0, x.dtype))
            weights = jax.nn.softmax(masked_logits / ROUTE_TEMP, axis=-1)
            top_vals, top_idx = jax.lax.top_k(weights, TOP_N)
            mask_oh = jax.nn.one_hot(top_idx, K, dtype=x.dtype).sum(axis=1)
            wm = weights * mask_oh
            wsel = wm / (wm.sum(axis=-1, keepdims=True) + 1e-09)
            x_mod = x * (1.0 + attn_map * scale * a)
            y = jnp.zeros_like(x)
            for e in range(K):
                ye = conv3x3(x_mod, We[e], be[e])
                y = y + wsel[:, e][:, None, None, None] * ye
            top1 = top_idx[:, 0]
            not_last = (top1 != K - 1).astype(x.dtype)
            delta = jax.nn.one_hot(top1, K, dtype=x.dtype) * not_last[:, None]
            allowed = jnp.clip(allowed - delta, 0.0, 1.0)
            allowed = jnp.maximum(allowed, last_oh)
            x = y
        return x

    def _L1_conv_ref(x, t_in_w, t_conv_w, t_conv_b, t_xproj_w, t_dt_w, t_dt_b, t_A_log, t_D, t_out_w, d_in_w, d_conv_w, d_conv_b, d_xproj_w, d_dt_w, d_dt_b, d_A_log, d_D, d_out_w):
        import jax, jax.numpy as jnp
        from jax import lax
        import numpy as np
        D_MODEL, D_STATE, D_CONV, EXPAND = (64, 16, 4, 2)
        D_INNER = EXPAND * D_MODEL
        DT_RANK = (D_MODEL + 15) // 16
        B, NVAR, SEG = (4, 32, 24)

        def _mamba_params(key, scale=0.02):
            ks = jax.random.split(key, 7)
            in_w = jax.random.normal(ks[0], (2 * D_INNER, D_MODEL)) * scale
            conv_w = jax.random.normal(ks[1], (D_INNER, D_CONV)) * scale
            conv_b = jnp.zeros((D_INNER,))
            xproj_w = jax.random.normal(ks[2], (DT_RANK + 2 * D_STATE, D_INNER)) * scale
            dt_w = jax.random.normal(ks[3], (D_INNER, DT_RANK)) * scale
            dt = jnp.exp(jax.random.uniform(ks[4], (D_INNER,)) * (np.log(0.1) - np.log(0.001)) + np.log(0.001))
            dt_b = dt + jnp.log(-jnp.expm1(-dt))
            A_log = jnp.log(jnp.broadcast_to(jnp.arange(1, D_STATE + 1, dtype=jnp.float32), (D_INNER, D_STATE)))
            Dvec = jnp.ones((D_INNER,))
            out_w = jax.random.normal(ks[5], (D_MODEL, D_INNER)) * scale
            return (in_w, conv_w, conv_b, xproj_w, dt_w, dt_b, A_log, Dvec, out_w)

        def _mamba(x, in_w, conv_w, conv_b, xproj_w, dt_w, dt_b, A_log, Dvec, out_w):
            Bn, L, _ = x.shape
            xz = jnp.einsum('bld,ed->ble', x, in_w)
            xi, z = jnp.split(xz, 2, axis=-1)
            xi_nc = xi.transpose(0, 2, 1)
            xc = lax.conv_general_dilated(xi_nc, conv_w[:, None, :], (1,), [(D_CONV - 1, 0)], feature_group_count=D_INNER)
            xc = jax.nn.silu(xc + conv_b[None, :, None]).transpose(0, 2, 1)
            dbl = jnp.einsum('ble,fe->blf', xc, xproj_w)
            dt, Bm, Cm = jnp.split(dbl, [DT_RANK, DT_RANK + D_STATE], axis=-1)
            dt = jax.nn.softplus(jnp.einsum('blr,er->ble', dt, dt_w) + dt_b)
            A = -jnp.exp(A_log)

            def step(h, inp):
                dt_t, B_t, C_t, u_t = inp
                dA = jnp.exp(dt_t[:, :, None] * A)
                h = dA * h + dt_t[:, :, None] * B_t[:, None, :] * u_t[:, :, None]
                y = jnp.einsum('bes,bs->be', h, C_t)
                return (h, y)
            h0 = jnp.zeros((Bn, D_INNER, D_STATE), x.dtype)
            _, ys = lax.scan(step, h0, (dt.transpose(1, 0, 2), Bm.transpose(1, 0, 2), Cm.transpose(1, 0, 2), xc.transpose(1, 0, 2)))
            y = ys.transpose(1, 0, 2) + xc * Dvec
            y = y * jax.nn.silu(z)
            return jnp.einsum('ble,de->bld', y, out_w)
        Bb, Dv, S, dm = x.shape
        xt = _mamba(x.reshape(Bb * Dv, S, dm), t_in_w, t_conv_w, t_conv_b, t_xproj_w, t_dt_w, t_dt_b, t_A_log, t_D, t_out_w)
        xt = xt.reshape(Bb, Dv, S, dm)
        xd = _mamba(xt.transpose(0, 2, 1, 3).reshape(Bb * S, Dv, dm), d_in_w, d_conv_w, d_conv_b, d_xproj_w, d_dt_w, d_dt_b, d_A_log, d_D, d_out_w)
        return xd.reshape(Bb, S, Dv, dm).transpose(0, 2, 1, 3)

    def _gn(v, G=32, eps=1e-05):
        B_, H_, W_, C_ = v.shape
        g = v.reshape(B_, H_, W_, G, C_ // G)
        m = jnp.mean(g, axis=(1, 2, 4), keepdims=True)
        s = jnp.var(g, axis=(1, 2, 4), keepdims=True)
        return ((g - m) / jnp.sqrt(s + eps)).reshape(v.shape)

    def _ln_c(v, eps=1e-06):
        m = jnp.mean(v, axis=-1, keepdims=True)
        s = jnp.var(v, axis=-1, keepdims=True)
        return (v - m) / jnp.sqrt(s + eps)

    def _ln_t(v, eps=1e-05):
        m = jnp.mean(v, axis=-1, keepdims=True)
        s = jnp.var(v, axis=-1, keepdims=True)
        return (v - m) / jnp.sqrt(s + eps)

    def _to_tokens(v):
        B_, H_, W_, C_ = v.shape
        return v.reshape(B_, H_ * W_, C_)

    def _from_tokens(t, like):
        return t.reshape(like.shape)
    x = x + _L0_conv_ref(_gn(x), L0_conv_q, L0_conv_Wk, L0_conv_Wv, L0_conv_Wmlp, L0_conv_alpha, L0_conv_We, L0_conv_be)
    x = x + _L1_conv_ref(_gn(x), L1_conv_t_in_w, L1_conv_t_conv_w, L1_conv_t_conv_b, L1_conv_t_xproj_w, L1_conv_t_dt_w, L1_conv_t_dt_b, L1_conv_t_A_log, L1_conv_t_D, L1_conv_t_out_w, L1_conv_d_in_w, L1_conv_d_conv_w, L1_conv_d_conv_b, L1_conv_d_xproj_w, L1_conv_d_dt_w, L1_conv_d_dt_b, L1_conv_d_A_log, L1_conv_d_D, L1_conv_d_out_w)
    return x

_drawn_inputs = setup_inputs


def setup_inputs(seed=0):
    import zlib

    import numpy as np

    out = dict(_drawn_inputs(seed))
    spreads = {'L0_conv_be': (0.0, 0.1),
     'L1_conv_t_conv_b': (0.0, 0.8),
     'L1_conv_t_D': (1.0, 0.6),
     'L1_conv_d_conv_b': (0.0, 0.8),
     'L1_conv_d_D': (1.0, 0.6)}
    factors = {'L1_conv_t_in_w': 8.0,
     'L1_conv_t_conv_w': 8.0,
     'L1_conv_t_xproj_w': 8.0,
     'L1_conv_t_out_w': 8.0,
     'L1_conv_d_in_w': 8.0,
     'L1_conv_d_conv_w': 8.0,
     'L1_conv_d_xproj_w': 8.0,
     'L1_conv_d_out_w': 8.0,
     'L1_conv_t_dt_w': 8.0,
     'L1_conv_d_dt_w': 8.0}
    for name, (base, spread) in spreads.items():
        noise = np.random.default_rng([zlib.crc32(name.encode()), seed]).standard_normal(out[name].shape)
        drawn = base * np.exp(spread * noise) if base else spread * noise
        out[name] = jnp.asarray(drawn.astype(out[name].dtype))
    for name, factor in factors.items():
        out[name] = (out[name] * factor).astype(out[name].dtype)
    return out
```

```python
from contextlib import ExitStack

import concourse.bass as bass
from concourse import mybir

IMAGES, SIDE, CH = 32, 32, 64
HEADS, DIM_HEAD, EXPERTS, STEPS = 2, 16, 4, 3
PIX = SIDE * SIDE // 2
ROWS2 = SIDE // 2
INNER, STATES, TAPS = 128, 16, 4
SEQS = PIX // SIDE
UNITS = IMAGES * 4
MAIN, ANTI = 3 * 128, 3 * 64
PHASES = 2 * STEPS


def build(nc, x_in, wk, q, wvT, wmlp, alpha, we, be, mamba_w, out, mid_x, mid_n):
    f32, bf16 = mybir.dt.float32, mybir.dt.bfloat16
    ACT, ALU = mybir.ActivationFunctionType, mybir.AluOpType
    X = mybir.AxisListType.X
    ctx = ExitStack()

    def sb(name, shape, dt=f32):
        return ctx.enter_context(nc.sbuf_tensor(name, shape, dt))

    def sem(name):
        return ctx.enter_context(nc.semaphore(name))

    with ctx:
        ident = sb("ident", [128, 128])
        neg_swap = sb("neg_swap", [128, 128])
        ones = sb("ones", [128, 128])
        group_mean = sb("group_mean", [128, 128])
        same_par = sb("same_par", [128, 128])
        select = sb("select", [128, 2 * STATES, 128], bf16)
        tie = sb("tie", [128, EXPERTS, EXPERTS])
        wk_sb = sb("wk_sb", [128, HEADS * DIM_HEAD])
        q_sb = sb("q_sb", [128, HEADS * DIM_HEAD])
        kq = sb("kq", [128, HEADS])
        score_w = sb("score_w", [128, HEADS, 128])
        wv_sb = sb("wv_sb", [DIM_HEAD, HEADS, 128])
        wmlp_sb = sb("wmlp_sb", [DIM_HEAD, HEADS, EXPERTS])
        route_w = sb("route_w", [128, HEADS, EXPERTS])
        gain = sb("gain", [128, 4])
        we_sb = sb("we_sb", [128, EXPERTS, MAIN + ANTI])
        be_sb = sb("be_sb", [128, EXPERTS])
        wi = [sb(f"wi{m}", [128, 2 * INNER]) for m in range(2)]
        wc = [sb(f"wc{m}", [128, TAPS]) for m in range(2)]
        wcb = [sb(f"wcb{m}", [128, 1]) for m in range(2)]
        wbc = [sb(f"wbc{m}", [128, 4, 2 * STATES]) for m in range(2)]
        wdt_in = [sb(f"wdt_in{m}", [4, 128]) for m in range(2)]
        wdt_out = [sb(f"wdt_out{m}", [4, 128]) for m in range(2)]
        wdt = [sb(f"wdt{m}", [128, 128]) for m in range(2)]
        wdtb = [sb(f"wdtb{m}", [128, 1]) for m in range(2)]
        wa = [sb(f"wa{m}", [128, STATES]) for m in range(2)]
        wd = [sb(f"wd{m}", [128, 1]) for m in range(2)]
        wo = [sb(f"wo{m}", [128, CH]) for m in range(2)]

        weights_loaded = sem("weights_loaded")
        const_memset = sem("const_memset")
        const_built = sem("const_built")
        kq_ready = sem("kq_ready")
        gain_act = sem("gain_act")
        small_products = sem("small_products")
        a_exp = sem("a_exp")
        dve_chain = sem("dve_chain")

        loads = [(wk_sb[:], wk), (wv_sb[:], wvT), (wmlp_sb[:], wmlp), (we_sb[:], we), (be_sb[:], be),
                 (q_sb[:], q.partition_broadcast(128)), (gain[:, 0:1], alpha.partition_broadcast(128))]
        for m in range(2):
            w = mamba_w[m]
            loads += [(wi[m][0:CH, :], w["in"]), (wi[m][CH:128, :], w["in"]), (wc[m][:], w["conv"]),
                      (wcb[m][:], w["conv_b"]), (wdt_in[m][:], w["dt_in"]), (wdt_out[m][:], w["dt_out"]),
                      (wdtb[m][:], w["dt_b"]), (wa[m][:], w["a_log"]), (wd[m][:], w["d"]), (wo[m][:], w["out"])]
            loads += [(wbc[m][:, r, :], w["bc"]) for r in range(4)]

        with ExitStack() as setup_ctx:
            p_setup = [setup_ctx.enter_context(nc.psum_tensor(f"p_setup{i}", [128, 512], f32)) for i in range(4)]
            block = setup_ctx.enter_context(nc.Block())

            @block.sync
            def _(sp):
                for dst, src in loads:
                    sp.dma_start(dst, src).then_inc(weights_loaded, 16)
                sp.wait_ge(weights_loaded, 16 * len(loads))

            @block.gpsimd
            def _(pool):
                def place(ap, fill, base, pattern, count):
                    nc.gpsimd.affine_select(out=ap, in_=ap, compare_op=ALU.not_equal, fill=fill, base=base,
                                            pattern=pattern, channel_multiplier=1).then_inc(const_built, 1)
                    pool.wait_ge(const_built, count)

                pool.wait_ge(const_memset, 5)
                place(ident[:], 1.0, 0, [[-1, 128]], 1)
                place(neg_swap[:, 0:64], -1.0, -64, [[-1, 64]], 2)
                place(neg_swap[:, 64:128], -1.0, 0, [[-1, 64]], 3)
                n = 3
                for off in (0, 1, 64, 65):
                    n += 1
                    place(group_mean[:].rearrange("p (a g k) -> p a g k", a=2, k=2), 0.25, -off,
                          [[0, 2], [-2, 32], [0, 2]], n)
                for off in (0, 64, 96):
                    n += 1
                    place(select[:], 1.0, -off, [[-1, 2 * STATES], [0, 128]], n)

            @block.vector
            def _(dve):
                nc.vector.memset(ident[:], 0.0).then_inc(const_memset, 1)
                nc.vector.memset(neg_swap[:], 0.0).then_inc(const_memset, 1)
                nc.vector.memset(group_mean[:], 0.0).then_inc(const_memset, 1)
                nc.vector.memset(select[:], 0.0).then_inc(const_memset, 1)
                nc.vector.memset(ones[:], 1.0).then_inc(const_memset, 1)
                nc.vector.memset(same_par[:], 0.0).then_inc(dve_chain, 1)
                nc.vector.memset(tie[:], 0.0).then_inc(dve_chain, 1)
                dve.wait_ge(dve_chain, 2)
                nc.vector.memset(same_par[0:64, 0:64], 1.0)
                nc.vector.memset(same_par[64:128, 64:128], 1.0).then_inc(dve_chain, 1)
                for e in range(1, EXPERTS):
                    nc.vector.memset(tie[:, e, 0:e], 1.0).then_inc(dve_chain, 1)
                dve.wait_ge(weights_loaded, 16 * len(loads))
                nc.vector.tensor_tensor(wk_sb[:], wk_sb[:], q_sb[:], ALU.mult).then_inc(dve_chain, 1)
                dve.wait_ge(dve_chain, 7)
                nc.vector.reduce_sum(kq[:], wk_sb[:].rearrange("p (n d) -> p n d", n=HEADS), X).then_inc(dve_chain, 1)
                dve.wait_ge(dve_chain, 8)
                for n in range(HEADS):
                    nc.vector.tensor_scalar(score_w[:, n, :], same_par[:], kq[:, n:n + 1], DIM_HEAD ** -0.5,
                                            ALU.mult, ALU.mult)
                nc.vector.tensor_scalar(gain[:, 2:3], gain[:, 0:1], 0.0, None, ALU.max).then_inc(dve_chain, 1)
                dve.wait_ge(dve_chain, 9)
                dve.wait_ge(gain_act, 3)
                nc.vector.tensor_tensor(gain[:, 3:4], gain[:, 1:2], gain[:, 2:3], ALU.add)
                dve.wait_ge(small_products, 4)
                for n in range(HEADS):
                    nc.vector.tensor_copy(route_w[:, n, :], p_setup[n][:, 0:EXPERTS])
                dve.wait_ge(a_exp, 2)
                for m in range(2):
                    nc.vector.tensor_copy(wdt[m][:], p_setup[2 + m][:, 0:128])
                    nc.vector.tensor_scalar(wa[m][:], wa[m][:], -1.0, None, ALU.mult)

            @block.scalar
            def _(act):
                act.wait_ge(weights_loaded, 16 * len(loads))
                nc.scalar.activation(gain[:, 1:2], gain[:, 0:1], ACT.Abs).then_inc(gain_act, 1)
                act.wait_ge(gain_act, 1)
                nc.scalar.activation(gain[:, 1:2], gain[:, 1:2], ACT.Exp, scale=-1.0).then_inc(gain_act, 1)
                act.wait_ge(gain_act, 2)
                nc.scalar.activation(gain[:, 1:2], gain[:, 1:2], ACT.Ln, bias=1.0).then_inc(gain_act, 1)
                for m in range(2):
                    nc.scalar.activation(wa[m][:], wa[m][:], ACT.Exp).then_inc(a_exp, 1)

            @block.tensor
            def _(pe):
                pe.wait_ge(weights_loaded, 16 * len(loads))
                for n in range(HEADS):
                    nc.tensor.matmul(p_setup[n][:, 0:EXPERTS], wv_sb[:, n, :], wmlp_sb[:, n, :],
                                     start=True, stop=True).then_inc(small_products, 1)
                for m in range(2):
                    nc.tensor.matmul(p_setup[2 + m][:, 0:128], wdt_in[m][:], wdt_out[m][:],
                                     start=True, stop=True).then_inc(small_products, 1)

        stage1(nc, x_in, mid_x, mid_n, dict(
            neg_swap=neg_swap, ones=ones, group_mean=group_mean, tie=tie, score_w=score_w, route_w=route_w,
            gain=gain, we=we_sb, be=be_sb))
        stage2(nc, mid_x, mid_n, out, dict(
            ident=ident, select=select, wi=wi, wc=wc, wcb=wcb, wbc=wbc, wdt=wdt, wdtb=wdtb, wa=wa, wd=wd, wo=wo))


def stage1(nc, x_in, mid_x, mid_n, c):
    f32 = mybir.dt.float32
    ACT, ALU = mybir.ActivationFunctionType, mybir.AluOpType
    X = mybir.AxisListType.X
    BODIES = IMAGES // 4
    LINKS = 190
    ctx = ExitStack()
    with ctx:
        def sb(name, shape, dt=f32):
            return ctx.enter_context(nc.sbuf_tensor(name, shape, dt))

        def sem(name):
            return ctx.enter_context(nc.semaphore(name))

        x0 = [[sb(f"x0_{g}{a}", [128, PIX]) for a in range(2)] for g in range(2)]
        xc = [[sb(f"xc_{g}{a}", [128, PIX]) for a in range(2)] for g in range(2)]
        x1 = [[sb(f"x1_{g}{a}", [128, PIX]) for a in range(2)] for g in range(2)]
        xn = [[sb(f"xn_{g}{a}", [128, PIX]) for a in range(2)] for g in range(2)]
        padded = [[sb(f"pad_{g}{a}", [128, ROWS2, SIDE + 2]) for a in range(2)] for g in range(2)]
        shifted = [[sb(f"shf_{g}{a}", [128, ROWS2, SIDE + 2]) for a in range(2)] for g in range(2)]
        w_main = [[sb(f"wm_{g}{a}", [128, 3, 128]) for a in range(2)] for g in range(2)]
        w_anti = [[sb(f"wx_{g}{a}", [128, 3, 128]) for a in range(2)] for g in range(2)]
        mix0 = [sb(f"mix0_{a}", [128, MAIN + ANTI]) for a in range(2)]
        mix1 = [sb(f"mix1_{a}", [128, MAIN + ANTI]) for a in range(2)]
        attn = [sb(f"attn_{a}", [128, HEADS, PIX]) for a in range(2)]
        modul = [sb(f"modul_{a}", [128, PIX]) for a in range(2)]
        scrap = sb("scrap", [128, HEADS, PIX])
        pool_scrap = sb("pool_scrap", [128, 1])
        pool_scrap2 = sb("pool_scrap2", [128, 1])
        stats = sb("stats", [128, 2, 6])
        moments = sb("moments", [128, 2, 2])
        gn = sb("gn", [128, 10, 2])
        hold = sb("hold", [128, 1])
        top = sb("top", [128, 2, HEADS])
        neg_top = sb("neg_top", [128, 2, HEADS])
        pooled = sb("pooled", [128, 2 * HEADS])
        parts = sb("parts", [128, 2 * HEADS * EXPERTS + 2 * HEADS])
        NP = 2 * HEADS * EXPERTS
        r = sb("r", [128, 2 * HEADS])
        logit_n = sb("logit_n", [128, 2, HEADS, EXPERTS])
        logit = sb("logit", [128, 2, EXPERTS])
        prob = sb("prob", [128, 2, EXPERTS])
        col = sb("col", [128, 6, 2])
        above = sb("above", [128, 2, EXPERTS, EXPERTS])
        equal = sb("equal", [128, 2, EXPERTS, EXPERTS])
        rank = sb("rank", [128, 2, EXPERTS])
        chosen = sb("chosen", [128, 2, EXPERTS])
        wsel = sb("wsel", [128, 2, EXPERTS])
        bias_e = sb("bias_e", [128, 2, EXPERTS])
        bias = [sb(f"bias_{g}", [128, 2]) for g in range(2)]
        allowed = [sb(f"allowed_{g}", [128, 2, EXPERTS]) for g in range(2)]
        penalty = [sb(f"penalty_{g}", [128, 2, EXPERTS]) for g in range(2)]
        kmap = sb("kmap", [128, 2 * HEADS])

        p_score = [ctx.enter_context(nc.psum_tensor(f"p_score{a}", [128, HEADS, 512], f32)) for a in range(2)]
        p_conv = [ctx.enter_context(nc.psum_tensor(f"p_conv{a}", [128, 512], f32)) for a in range(2)]
        p_small = ctx.enter_context(nc.psum_tensor("p_small", [128, 512], f32))
        P_SWAP, P_SUM, P_MEAN, P_VAR = (slice(0, 4), slice(16, 16 + NP + 4), slice(64, 66), slice(80, 82))

        loaded_x = sem("s1_loaded_x")
        loaded_y = sem("s1_loaded_y")
        stored_x = sem("s1_stored_x")
        stored_y = sem("s1_stored_y")
        gn_mean_in = sem("s1_gn_mean_in")
        gn_mean = sem("s1_gn_mean")
        gn_var_in = sem("s1_gn_var_in")
        gn_var = sem("s1_gn_var")
        gn_v = sem("s1_gn_v")
        gn_ln = sem("s1_gn_ln")
        gn_rs = sem("s1_gn_rs")
        x_norm = sem("s1_x_norm")
        x_out = sem("s1_x_out")
        x_step = sem("s1_x_step")
        score_done = sem("s1_score_done")
        top_ready = sem("s1_top_ready")
        swap_done = sem("s1_swap_done")
        neg_top_ready = sem("s1_neg_top_ready")
        exp_done = sem("s1_exp_done")
        parts_ready = sem("s1_parts_ready")
        sum_done = sem("s1_sum_done")
        wexp_in = sem("s1_wexp_in")
        wexp_done = sem("s1_wexp_done")
        wsel_ready = sem("s1_wsel_ready")
        mix01 = sem("s1_mix01")
        mix_ready = sem("s1_mix_ready")
        w_ready = sem("s1_w_ready")
        modul_ready = sem("s1_modul_ready")
        padded_ready = sem("s1_padded_ready")
        shifted_ready = sem("s1_shifted_ready")
        w_main_done, w_even_done = sem("s1_w_main_done"), sem("s1_w_even_done")
        shifted_even_done = sem("s1_shifted_even_done")
        conv_done = sem("s1_conv_done")
        zeroed = sem("s1_zeroed")
        zeroed_dve = sem("s1_zeroed_dve")
        x1_ready = sem("s1_x1_ready")
        link = sem("s1_link")

        block = ctx.enter_context(nc.Block())

        @block.sync
        def _(sp):
            fetched, done = (loaded_x, loaded_y), (stored_x, stored_y)

            def fetch(body, g):
                for a in range(2):
                    sp.dma_start(x0[g][a][:], x_in[4 * body + 2 * g + a]).then_inc(fetched[g], 16)

            def store(body, g):
                sp.wait_ge(x_out, 2 * body + g + 1)
                for a in range(2):
                    sp.dma_start(mid_x[4 * body + 2 * g + a], x1[g][a][:]).then_inc(done[g], 16)
                    sp.dma_start(mid_n[4 * body + 2 * g + a], xn[g][a][:]).then_inc(done[g], 16)

            for g in range(2):
                fetch(0, g)
            with sp.Fori(0, BODIES - 1) as i:
                for g in range(2):
                    store(i, g)
                    sp.wait_ge(done[g], 64 * i + 64)
                    fetch(i + 1, g)
            for g in range(2):
                store(BODIES - 1, g)
                sp.wait_ge(done[g], 64 * BODIES)

        @block.tensor
        def _(pe):
            def group_sums(n):
                pe.wait_ge(gn_mean_in, n + 1)
                nc.tensor.matmul(p_small[:, P_MEAN], c["group_mean"][:], moments[:, :, 0],
                                 start=True, stop=True).then_inc(gn_mean, 1)
                pe.wait_ge(gn_var_in, n + 1)
                nc.tensor.matmul(p_small[:, P_VAR], c["group_mean"][:], gn[:, 2, :],
                                 start=True, stop=True).then_inc(gn_var, 1)

            def score(i, k):
                g, t = k % 2, k // 2
                for a in range(2):
                    if t == 0:
                        pe.wait_ge(x_norm, 2 * i + g + 1)
                    else:
                        pe.wait_ge(x_step, i * 8 + 2 * (k - 2) + a + 1)
                    for n in range(HEADS):
                        mm = nc.tensor.matmul(p_score[a][:, n, :], c["score_w"][:, n, :], xc[g][a][:],
                                              start=True, stop=True)
                    mm.then_inc(score_done, 1)

            def swap(i, k):
                pe.wait_ge(top_ready, i * PHASES + k + 1)
                nc.tensor.matmul(p_small[:, P_SWAP], c["neg_swap"][:], top[:].rearrange("p a n -> p (a n)"),
                                 start=True, stop=True).then_inc(swap_done, 1)

            def total(i, k):
                pe.wait_ge(parts_ready, i * PHASES + k + 1)
                nc.tensor.matmul(p_small[:, P_SUM], c["ones"][:], parts[:],
                                 start=True, stop=True).then_inc(sum_done, 1)

            def conv(i, k, a):
                g = k % 2
                P = i * PHASES + k
                pe.wait_ge(w_ready, 2 * P + a + 3)
                pe.wait_ge(padded_ready, 2 * P + a + 1)
                pe.wait_ge(shifted_ready, 2 * P + a + 3)
                if 1 <= k <= PHASES - 2:
                    pe.wait_ge(x_step, i * 8 + 2 * (k - 1) + a + 1)
                elif k == PHASES - 1:
                    pe.wait_ge(x1_ready, 4 * i + a + 1)
                n = 0
                for w, src in ((w_main, padded), (w_anti, shifted)):
                    for dx in range(3):
                        mm = nc.tensor.matmul(p_conv[a][:], w[g][a][:, dx, :], src[g][a][:, :, dx:dx + SIDE],
                                              start=(n == 0), stop=(n == 5))
                        n += 1
                mm.then_inc(conv_done, 1)

            with pe.Fori(0, BODIES) as i:
                group_sums(4 * i)
                score(i, 0)
                group_sums(4 * i + 1)
                for k in range(PHASES):
                    swap(i, k)
                    if k:
                        conv(i, k - 1, 0)
                    total(i, k)
                    if k:
                        conv(i, k - 1, 1)
                    if k + 1 < PHASES:
                        score(i, k + 1)
                group_sums(4 * i + 2)
                conv(i, PHASES - 1, 0)
                conv(i, PHASES - 1, 1)
                group_sums(4 * i + 3)

        @block.scalar
        def _(act):
            def group_root(n):
                act.wait_ge(gn_v, n + 1)
                nc.scalar.activation(gn[:, 4, :], gn[:, 3, :], ACT.Ln).then_inc(gn_ln, 1)
                act.wait_ge(gn_ln, n + 1)
                nc.scalar.activation(gn[:, 5, :], gn[:, 4, :], ACT.Exp, scale=-0.5).then_inc(gn_rs, 1)

            def step_out(i, k):
                g = k % 2
                for a in range(2):
                    act.wait_ge(conv_done, (i * PHASES + k) * 2 + a + 1)
                    nc.scalar.activation(xc[g][a][:], p_conv[a][:], ACT.Identity,
                                         bias=bias[g][:, a:a + 1]).then_inc(x_step, 1)

            nc.scalar.preload_act_table_set("natural_log_exp_and_others")
            with act.Fori(0, BODIES) as i:
                group_root(4 * i)
                group_root(4 * i + 1)
                for k in range(PHASES):
                    P = i * PHASES + k
                    act.wait_ge(neg_top_ready, P + 1)
                    for a in range(2):
                        for n in range(HEADS):
                            ex = nc.scalar.activation(attn[a][:, n, :], p_score[a][:, n, :], ACT.Exp,
                                                      bias=neg_top[:, a, n:n + 1],
                                                      accum_out=parts[:, NP + 2 * a + n:NP + 2 * a + n + 1])
                        ex.then_inc(exp_done, 1)
                    act.wait_ge(wexp_in, P + 1)
                    nc.scalar.activation(prob[:], logit[:], ACT.Exp, scale=1.0 / 1.5).then_inc(wexp_done, 1)
                    if 1 <= k <= PHASES - 2:
                        step_out(i, k - 1)
                    act.wait_ge(wsel_ready, P + 1)
                    for a in range(2):
                        act.wait_ge(w_ready, 2 * P + a + 1)
                        nc.scalar.mul(mix0[a][:], c["we"][:, 0, :], wsel[:, a, 0:1])
                        nc.scalar.mul(mix1[a][:], c["we"][:, 1, :], wsel[:, a, 1:2]).then_inc(mix01, 1)
                group_root(4 * i + 2)
                group_root(4 * i + 3)

        @block.gpsimd
        def _(pool):
            for g in range(2):
                for a in range(2):
                    nc.gpsimd.memset(w_anti[g][a][:], 0.0).then_inc(zeroed, 1)
                    nc.gpsimd.memset(shifted[g][a][:], 0.0).then_inc(zeroed, 1)
            pool.wait_ge(zeroed, 8)
            nc.gpsimd.memset(pool_scrap[:], 0.0).then_inc(w_ready, 2)
            nc.gpsimd.memset(pool_scrap2[:], 0.0).then_inc(shifted_ready, 2)
            with pool.Fori(0, BODIES) as i:
                for k in range(PHASES):
                    g, P = k % 2, i * PHASES + k
                    for a in range(2):
                        pool.wait_ge(mix_ready, 2 * P + a + 1)
                        nc.gpsimd.tensor_tensor(w_main[g][a][:].rearrange("p d c -> p (d c)"), mix0[a][:, 0:MAIN],
                                                mix1[a][:, 0:MAIN], ALU.add).then_inc(w_main_done, 1)
                        pool.wait_ge(w_main_done, 2 * P + a + 1)
                        for par in range(2):
                            rows, cols = slice(64 * par, 64 * par + 64), slice(64 - 64 * par, 128 - 64 * par)
                            nc.gpsimd.tensor_tensor(
                                w_anti[g][a][rows, :, cols],
                                mix0[a][rows, MAIN:].rearrange("p (d c) -> p d c", d=3),
                                mix1[a][rows, MAIN:].rearrange("p (d c) -> p d c", d=3),
                                ALU.add).then_inc((w_even_done, w_ready)[par], 1)
                            pool.wait_ge((w_even_done, w_ready)[par], 2 * P + a + 1 + 2 * par)
                    for a in range(2):
                        pool.wait_ge(modul_ready, 2 * P + a + 1)
                        m3 = modul[a][:].rearrange("p (j w) -> p j w", j=ROWS2)
                        x3 = xc[g][a][:].rearrange("p (j w) -> p j w", j=ROWS2)
                        nc.gpsimd.tensor_tensor(shifted[g][a][0:64, 0:ROWS2 - 1, 1:SIDE + 1], m3[0:64, 1:, :],
                                                x3[0:64, 1:, :], ALU.mult).then_inc(shifted_even_done, 1)
                        pool.wait_ge(shifted_even_done, 2 * P + a + 1)
                        nc.gpsimd.tensor_tensor(shifted[g][a][64:128, 1:ROWS2, 1:SIDE + 1], m3[64:128, :ROWS2 - 1, :],
                                                x3[64:128, :ROWS2 - 1, :], ALU.mult).then_inc(shifted_ready, 1)
                        if a == 0 or k < PHASES - 1:
                            pool.wait_ge(shifted_ready, 2 * P + a + 3)

        @block.vector
        def _(dve):
            n_links = [0, None]

            def chain(ins):
                n_links[0] += 1
                ins.then_inc(link, 1)
                dve.wait_ge(link, n_links[1] + n_links[0])

            def group_norm(n, src, dst, finish):
                for a in range(2):
                    st = nc.vector.bn_stats(stats[:, a, :], src[a][:])
                chain(st)
                nc.vector.memset(hold[:], 0.0)
                for a in range(2):
                    ag = nc.vector.bn_aggr(moments[:, a, :], stats[:, a, :])
                ag.then_inc(gn_mean_in, 1)
                dve.wait_ge(gn_mean, n + 1)
                chain(nc.vector.tensor_copy(gn[:, 0, :], p_small[:, P_MEAN]))
                chain(nc.vector.tensor_tensor(gn[:, 1, :], moments[:, :, 0], gn[:, 0, :], ALU.subtract))
                chain(nc.vector.tensor_tensor(gn[:, 2, :], gn[:, 1, :], gn[:, 1, :], ALU.mult))
                nc.vector.tensor_tensor(gn[:, 2, :], gn[:, 2, :], moments[:, :, 1], ALU.add).then_inc(gn_var_in, 1)
                dve.wait_ge(gn_var, n + 1)
                nc.vector.tensor_scalar(gn[:, 3, :], p_small[:, P_VAR], 1e-5, None, ALU.add).then_inc(gn_v, 1)
                dve.wait_ge(gn_rs, n + 1)
                for src_r, dst_r in ((5, 8), (8, 9)):
                    chain(nc.vector.tensor_tensor(gn[:, 6, :], gn[:, src_r, :], gn[:, src_r, :], ALU.mult))
                    chain(nc.vector.tensor_tensor(gn[:, 6, :], gn[:, 6, :], gn[:, 3, :], ALU.mult))
                    chain(nc.vector.tensor_scalar(gn[:, 6, :], gn[:, 6, :], -0.5, 1.5, ALU.mult, ALU.add))
                    chain(nc.vector.tensor_tensor(gn[:, dst_r, :], gn[:, 6, :], gn[:, src_r, :], ALU.mult))
                for a in range(2):
                    o = nc.vector.tensor_scalar(dst[a][:], src[a][:], gn[:, 0, a:a + 1], gn[:, 9, a:a + 1],
                                                ALU.subtract, ALU.mult)
                o.then_inc(finish, 1)

            def step_last(i, g):
                k = 2 * (STEPS - 1) + g
                for a in range(2):
                    dve.wait_ge(conv_done, (i * PHASES + k) * 2 + a + 1)
                    o = nc.vector.scalar_tensor_tensor(x1[g][a][:], p_conv[a][:], bias[g][:, a:a + 1], x0[g][a][:],
                                                       ALU.add, ALU.add).then_inc(x1_ready, 1)
                dve.wait_ge(x1_ready, 4 * i + 2 * g + 2)

            def phase(i, k):
                g, t = k % 2, k // 2
                P = i * PHASES + k
                if t == 0:
                    nc.vector.memset(allowed[g][:], 1.0)
                    chain(nc.vector.memset(penalty[g][:], 0.0))
                for a in range(2):
                    dve.wait_ge(score_done, 2 * P + a + 1)
                    m = nc.vector.reduce_max(top[:, a, :], p_score[a][:], X)
                m.then_inc(top_ready, 1)
                dve.wait_ge(swap_done, P + 1)
                nc.vector.scalar_tensor_tensor(neg_top[:].rearrange("p a n -> p (a n)"),
                                               top[:].rearrange("p a n -> p (a n)"), -1.0, p_small[:, P_SWAP],
                                               ALU.mult, ALU.min).then_inc(neg_top_ready, 1)
                for a in range(2):
                    dve.wait_ge(exp_done, 2 * P + a + 1)
                    for n in range(HEADS):
                        pl = nc.vector.tensor_tensor_reduce(
                            out=scrap[:, n, :], in0=attn[a][:, n, :], in1=xc[g][a][:], scale=1.0, scalar=0.0,
                            op0=ALU.mult, op1=ALU.add, accum_out=pooled[:, 2 * a + n:2 * a + n + 1])
                    chain(pl)
                for a in range(2):
                    pt = nc.vector.tensor_tensor(
                        parts[:, 8 * a:8 * a + 8].rearrange("p (n e) -> p n e", n=HEADS), c["route_w"][:],
                        pooled[:, 2 * a:2 * a + 2].unsqueeze(2).broadcast_to([128, HEADS, EXPERTS]), ALU.mult)
                pt.then_inc(parts_ready, 1)
                dve.wait_ge(sum_done, P + 1)
                chain(nc.vector.reciprocal(r[:], p_small[:, 16 + NP:16 + NP + 4]))
                nc.vector.tensor_scalar(kmap[:], r[:], float(CH * PIX), c["gain"][:, 3:4], ALU.mult, ALU.mult)
                chain(nc.vector.tensor_tensor(
                    logit_n[:].rearrange("p a n e -> p (a n) e"), p_small[:, 16:16 + NP].rearrange("p (m e) -> p m e", e=4),
                    r[:].unsqueeze(2).broadcast_to([128, 4, EXPERTS]), ALU.mult))
                chain(nc.vector.tensor_tensor(logit[:], logit_n[:, :, 0, :], logit_n[:, :, 1, :], ALU.add))
                chain(nc.vector.scalar_tensor_tensor(logit[:], logit[:], float(CH), allowed[g][:], ALU.mult, ALU.mult))
                chain(nc.vector.tensor_tensor(logit[:], logit[:], penalty[g][:], ALU.add))
                chain(nc.vector.reduce_max(col[:, 0, :], logit[:], X))

                def per_image(j):
                    return col[:, j, :].unsqueeze(2).broadcast_to([128, 2, EXPERTS])

                nc.vector.tensor_tensor(logit[:], logit[:], per_image(0), ALU.subtract).then_inc(wexp_in, 1)
                dve.wait_ge(wexp_done, P + 1)
                chain(nc.vector.reduce_sum(col[:, 1, :], prob[:], X))
                chain(nc.vector.reciprocal(col[:, 2, :], col[:, 1, :]))
                chain(nc.vector.tensor_tensor(prob[:], prob[:], per_image(2), ALU.mult))
                w_e = prob[:].unsqueeze(3).broadcast_to([128, 2, EXPERTS, EXPERTS])
                w_j = prob[:].unsqueeze(2).broadcast_to([128, 2, EXPERTS, EXPERTS])
                nc.vector.tensor_tensor(above[:], w_j, w_e, ALU.is_gt)
                chain(nc.vector.tensor_tensor(equal[:], w_j, w_e, ALU.is_equal))
                chain(nc.vector.tensor_tensor(equal[:], equal[:],
                                              c["tie"][:].unsqueeze(1).broadcast_to([128, 2, EXPERTS, EXPERTS]), ALU.mult))
                chain(nc.vector.tensor_tensor(above[:], above[:], equal[:], ALU.add))
                chain(nc.vector.reduce_sum(rank[:], above[:], X))
                chain(nc.vector.scalar_tensor_tensor(chosen[:], rank[:], 1.5, prob[:], ALU.is_lt, ALU.mult))
                chain(nc.vector.reduce_sum(col[:, 3, :], chosen[:], X))
                chain(nc.vector.tensor_scalar(col[:, 4, :], col[:, 3, :], 1e-9, None, ALU.add))
                chain(nc.vector.reciprocal(col[:, 5, :], col[:, 4, :]))
                nc.vector.tensor_tensor(wsel[:], chosen[:], per_image(5), ALU.mult).then_inc(wsel_ready, 1)
                for a in range(2):
                    dve.wait_ge(shifted_ready, 2 * P + a + 1)
                    chain(nc.vector.tensor_scalar(modul[a][:], attn[a][:, 0, :], kmap[:, 2 * a:2 * a + 1], 1.0,
                                                  ALU.mult, ALU.add))
                    nc.vector.scalar_tensor_tensor(modul[a][:], attn[a][:, 1, :], kmap[:, 2 * a + 1:2 * a + 2],
                                                   modul[a][:], ALU.mult, ALU.add).then_inc(modul_ready, 1)
                    dve.wait_ge(modul_ready, 2 * P + a + 1)
                    nc.vector.tensor_tensor(padded[g][a][:, :, 1:SIDE + 1],
                                            modul[a][:].rearrange("p (j w) -> p j w", j=ROWS2),
                                            xc[g][a][:].rearrange("p (j w) -> p j w", j=ROWS2),
                                            ALU.mult).then_inc(padded_ready, 1)
                dve.wait_ge(wsel_ready, P + 1)
                chain(nc.vector.tensor_tensor(bias_e[:], wsel[:],
                                              c["be"][:].unsqueeze(1).broadcast_to([128, 2, EXPERTS]), ALU.mult))
                nc.vector.reduce_sum(bias[g][:], bias_e[:], X)
                for a in range(2):
                    dve.wait_ge(mix01, 2 * P + a + 1)
                    nc.vector.scalar_tensor_tensor(mix0[a][:], c["we"][:, 2, :], wsel[:, a, 2:3], mix0[a][:],
                                                   ALU.mult, ALU.add)
                    nc.vector.scalar_tensor_tensor(mix1[a][:], c["we"][:, 3, :], wsel[:, a, 3:4], mix1[a][:],
                                                   ALU.mult, ALU.add).then_inc(mix_ready, 1)
                if t < STEPS - 1:
                    chain(nc.vector.scalar_tensor_tensor(allowed[g][:, :, 0:3], rank[:, :, 0:3], 0.5,
                                                         allowed[g][:, :, 0:3], ALU.is_gt, ALU.mult))
                    chain(nc.vector.tensor_scalar(penalty[g][:], allowed[g][:], -1.0, 1e9, ALU.add, ALU.mult))

            for g in range(2):
                for a in range(2):
                    nc.vector.memset(padded[g][a][:], 0.0).then_inc(zeroed_dve, 1)
            dve.wait_ge(zeroed_dve, 4)
            with dve.Fori(0, BODIES) as i:
                n_links[0], n_links[1] = 0, i * LINKS
                for g in range(2):
                    dve.wait_ge((loaded_x, loaded_y)[g], 32 * i + 32)
                    group_norm(4 * i + g, x0[g], xc[g], x_norm)
                for k in range(PHASES):
                    phase(i, k)
                for g in range(2):
                    step_last(i, g)
                    group_norm(4 * i + 2 + g, x1[g], xn[g], x_out)
                assert n_links[0] == LINKS, n_links[0]


def stage2(nc, mid_x, mid_n, out, c):
    f32, bf16 = mybir.dt.float32, mybir.dt.bfloat16
    ACT, ALU = mybir.ActivationFunctionType, mybir.AluOpType
    ident, select, wi, wc, wcb, wbc, wdt, wdtb, wa, wd, wo = (
        c[k] for k in ("ident", "select", "wi", "wc", "wcb", "wbc", "wdt", "wdtb", "wa", "wd", "wo"))
    N = STATES
    HALF = SIDE // 2
    ROWS, COLS = 0, 1
    BODIES = IMAGES - 2
    LAG = 3
    AHEAD = 2
    AT = dict(skip=3, gate=3, project_out=5, leave_rows=6, leave_cols=6, hold_rows=0,
              project_in=1, copy_xi=2, taps=3, silus=7, project_dt_bc=9, softplus=10, relu_and_rest=11,
              second_part=12, make_dt=13, dtx=14)

    ctx = ExitStack()
    with ctx:
        def sb(name, shape, dt=f32):
            return ctx.enter_context(nc.sbuf_tensor(name, shape, dt))

        def ps(name):
            return ctx.enter_context(nc.psum_tensor(name, [128, 512], f32))

        def sem(name):
            return ctx.enter_context(nc.semaphore(name))

        norm_in = sb("norm_in", [128, PIX])
        resid = sb("resid", [128, PIX])
        rows_out = sb("rows_out", [128, SIDE, ROWS2])
        cols_in = sb("cols_in", [128, SIDE, ROWS2])
        result = sb("result", [128, ROWS2, SIDE])
        two, four = range(2), range(4)
        xi = sb("xi", [128, SEQS, SIDE])
        gate = [sb(f"gate{b}", [128, PIX]) for b in two]
        xconv = [sb(f"xconv{b}", [128, PIX]) for b in two]
        soft = sb("soft", [128, PIX])
        relu = sb("relu", [128, PIX])
        dt = [sb(f"dt{b}", [128, SEQS, SIDE]) for b in two]
        dtx = [sb(f"dtx{b}", [128, PIX]) for b in two]
        parts = [sb(f"bcparts{b}", [128, PIX], bf16) for b in two]
        rest = sb("rest", [128, PIX])
        drive = [sb(f"drive{b}", [128, PIX]) for b in four]
        decays = [sb(f"decays{b}", [128, PIX]) for b in four]
        state = [sb(f"state{b}", [128, PIX]) for b in four]
        c_sb = [sb(f"c_sb{b}", [128, PIX]) for b in four]
        read = [sb(f"read{b}", [128, PIX]) for b in four]
        y_skip = [sb(f"y_skip{b}", [128, PIX]) for b in two]
        gated = [sb(f"gated{b}", [128, PIX]) for b in two]

        p_a, p_b = ps("p_a"), ps("p_b")
        p_B = [ps("p_B0"), ps("p_B1")]
        p_C = [ps("p_C0"), ps("p_C1")]
        p_y = [ps("p_y0"), ps("p_y1")]

        norm_loaded = sem("norm_loaded")
        resid_loaded = sem("resid_loaded")
        out_stored = sem("out_stored")
        xz_done = sem("xz_done")
        even_in = sem("even_in")
        xi_copied = sem("xi_copied")
        tap0_done = sem("tap0_done")
        taps_done = sem("taps_done")
        gate_ready = sem("gate_ready")
        xconv_ready = sem("xconv_ready")
        dtraw_done = sem("dtraw_done")
        bc_done = sem("bc_done")
        soft_steps = sem("soft_steps")
        relu_done = sem("relu_done")
        dt_ready = sem("dt_ready")
        dtx_ready = sem("dtx_ready")
        part_copied = sem("part_copied")
        rest_ready = sem("rest_ready")
        parts_ready = sem("parts_ready")
        b_done = sem("b_done")
        c_done = sem("c_done")
        c_copied = sem("c_copied")
        decay_done = sem("decay_done")
        drive_done = sem("drive_done")
        scan_done = sem("scan_done")
        read_done = sem("read_done")
        y_added = sem("y_added")
        skip_done = sem("skip_done")
        gated_done = sem("gated_done")
        proj_done = sem("proj_done")
        left = sem("left")
        cols_ready = sem("cols_ready")
        decay_zeroed = sem("decay_zeroed")

        def ge(eng, s, value):
            if not isinstance(value, int) or value > 0:
                eng.wait_ge(s, value)

        def each_unit(eng, slot):
            first = [(ROWS, v % 2, v // 2) for v in range(4)]
            last = [(COLS, v % 2, IMAGES - 2 + v // 2) for v in range(4)]

            def around(i):
                return [(ROWS, 1, i + 1), (COLS, 0, i), (COLS, 1, i), (ROWS, 0, i + 2), (ROWS, 1, i + 2),
                        (COLS, 0, i + 1)]

            for v in range(4):
                slot(v, v % 2, first[v - 1] if v else None, first[v], (first + [(COLS, 0, 0)])[v + 1])
            with eng.Fori(0, BODIES) as i:
                units = around(i)
                for v in range(4):
                    slot(4 + 4 * i + v, v % 2, units[v], units[v + 1], units[v + 2])
            for v in range(4):
                slot(UNITS - 4 + v, v % 2, last[v - 1] if v else (ROWS, 1, IMAGES - 1), last[v],
                     last[v + 1] if v < 3 else None)

        block = ctx.enter_context(nc.Block())

        @block.sync
        def _(sp):
            sp.dma_start(norm_in[:], mid_n[0]).then_inc(norm_loaded, 16)
            sp.dma_start(resid[:], mid_x[0]).then_inc(resid_loaded, 16)
            for n in (1, 2):
                sp.wait_ge(xz_done, 2 * n)
                sp.dma_start(norm_in[:], mid_n[n]).then_inc(norm_loaded, 16)
            with sp.Fori(0, BODIES - 1) as i:
                sp.wait_ge(left, 4 * i + 6)
                sp.dma_start(out[i], result[:].rearrange("p j w -> p (j w)")).then_inc(out_stored, 16)
                sp.wait_ge(xz_done, 4 * i + 8)
                sp.dma_start(norm_in[:], mid_n[i + 3]).then_inc(norm_loaded, 16)
                sp.wait_ge(out_stored, 16 * i + 16)
                sp.dma_start(resid[:], mid_x[i + 1]).then_inc(resid_loaded, 16)
            for n in range(BODIES - 1, IMAGES):
                sp.wait_ge(left, 4 * n + 6 if n < IMAGES - 1 else UNITS)
                sp.dma_start(out[n], result[:].rearrange("p j w -> p (j w)")).then_inc(out_stored, 16)
                sp.wait_ge(out_stored, 16 * (n + 1))
                if n < IMAGES - 1:
                    sp.dma_start(resid[:], mid_x[n + 1]).then_inc(resid_loaded, 16)

        @block.tensor
        def _(pe):
            def project_in(u, unit):
                m, half, image = unit
                if m == ROWS:
                    pe.wait_ge(norm_loaded, 16 * image + 16)
                else:
                    pe.wait_ge(cols_ready, image + 1)
                ge(pe, rest_ready, u)
                x_cols, z_cols = slice(0, INNER), slice(INNER, 2 * INNER)
                if m == ROWS:
                    par = slice(CH * half, CH * half + CH)
                    nc.tensor.matmul(p_a[:], wi[0][par, x_cols], norm_in[par, :], start=True, stop=True)
                    ge(pe, relu_done, u)
                    ge(pe, soft_steps, 3 * u - 2)
                    nc.tensor.matmul(p_b[:], wi[0][par, z_cols], norm_in[par, :],
                                     start=True, stop=True).then_inc(xz_done, 1)
                else:
                    ge(pe, relu_done, u)
                    ge(pe, soft_steps, 3 * u - 2)
                    for p in two:
                        par = slice(CH * p, CH * p + CH)
                        rows_in = cols_in[par, HALF * half:HALF * half + HALF, :]
                        if p:
                            pe.wait_ge(even_in, 2 * image + half + 1)
                        nc.tensor.matmul(p_a[:, 256 * p:256 * p + 256], wi[1][par, x_cols], rows_in,
                                         start=True, stop=True)
                        nc.tensor.matmul(p_b[:, 256 * p:256 * p + 256], wi[1][par, z_cols], rows_in,
                                         start=True, stop=True).then_inc((even_in, xz_done)[p], 1)

            def project_dt_bc(u, b, unit):
                m = unit[0]
                pe.wait_ge(gate_ready, u + 1)
                pe.wait_ge(xconv_ready, u + 1)
                nc.tensor.matmul(p_a[:], wbc[m][:].rearrange("p a n -> p (a n)"), xconv[b][:],
                                 start=True, stop=True).then_inc(bc_done, 1)
                nc.tensor.matmul(p_b[:], wdt[m][:], xconv[b][:], start=True, stop=True).then_inc(dtraw_done, 1)

            def spread(u, b, s):
                if s == 0:
                    pe.wait_ge(parts_ready, u + 1)
                ge(pe, drive_done, N * u + s - 1)
                nc.tensor.matmul(p_B[s % 2][:], select[:, s, :], parts[b][:], start=True, stop=True).then_inc(b_done, 1)
                ge(pe, c_copied, N * u + s - 1)
                nc.tensor.matmul(p_C[s % 2][:], select[:, N + s, :], parts[b][:], start=True, stop=True).then_inc(c_done, 1)

            def add_state(u, b, s):
                if s == 0:
                    ge(pe, left, u - 1)
                pe.wait_ge(read_done, N * u + s + 1)
                nc.tensor.matmul(p_y[b][:], ident[:], read[s % 4][:], start=(s == 0), stop=(s == N - 1)).then_inc(y_added, 1)

            def project_out(u, b, unit):
                m, half, _ = unit
                pe.wait_ge(gated_done, u + 1)
                if m == ROWS:
                    mm = nc.tensor.matmul(p_y[b][CH * half:CH * half + CH, :], wo[0][:], gated[b][:],
                                          start=True, stop=True)
                else:
                    by_parity = gated[b][:].rearrange("p (n r) -> p n r", r=2)
                    for p in two:
                        mm = nc.tensor.matmul(p_y[b][CH * p:CH * p + CH, 0:256], wo[1][:], by_parity[:, :, p],
                                              start=True, stop=True)
                mm.then_inc(proj_done, 1)

            def slot(u, b, before, unit, after):
                for s in range(N):
                    spread(u, b, s)
                    if s >= LAG:
                        add_state(u, b, s - LAG)
                    elif before:
                        add_state(u - 1, 1 - b, N - LAG + s)
                    if s == AT["project_out"] and before:
                        project_out(u - 1, 1 - b, before)
                    if s == AT["project_in"] and after:
                        project_in(u + 1, after)
                    if s == AT["project_dt_bc"] and after:
                        project_dt_bc(u + 1, 1 - b, after)

            project_in(0, (ROWS, 0, 0))
            project_dt_bc(0, 0, (ROWS, 0, 0))
            each_unit(pe, slot)
            for s in range(N - LAG, N):
                add_state(UNITS - 1, 1, s)
            project_out(UNITS - 1, 1, (COLS, 1, IMAGES - 1))

        @block.scalar
        def _(act):
            def in_order(bank, m):
                if m == ROWS:
                    return bank[:].rearrange("p (q t) -> p q t", t=SIDE)
                return bank[:].rearrange("p (r w j) -> p w j r", r=2, w=HALF)

            def same_shape(ap, m):
                if m == ROWS:
                    return ap.rearrange("p (q t) -> p q t", t=SIDE)
                return ap.rearrange("p (w j r) -> p w j r", w=HALF, r=2)

            def copy_xi(u, m):
                act.wait_ge(xz_done, u + 1)
                nc.scalar.copy(same_shape(xi[:].rearrange("p q t -> p (q t)"), m), in_order(p_a, m)).then_inc(xi_copied, 1)
                act.wait_ge(xi_copied, u + 1)
                nc.scalar.activation(p_a[:], xi[:].rearrange("p q t -> p (q t)"), ACT.Identity,
                                     bias=wcb[m][:], scale=wc[m][:, TAPS - 1:TAPS]).then_inc(tap0_done, 1)

            def silus(u, b, m):
                ge(act, gated_done, u - 1)
                nc.scalar.activation(same_shape(gate[b][:], m), in_order(p_b, m), ACT.Silu).then_inc(gate_ready, 1)
                act.wait_ge(taps_done, 3 * u + 3)
                ge(act, skip_done, u - 1)
                nc.scalar.activation(xconv[b][:], p_a[:], ACT.Silu).then_inc(xconv_ready, 1)

            def exp_ln_tables():
                nc.scalar.preload_act_table_set("natural_log_exp_and_others")

            def first_part(u, b):
                act.wait_ge(bc_done, u + 1)
                ge(act, c_done, N * (u - 1))
                nc.scalar.copy(parts[b][:], p_a[:]).then_inc(part_copied, 1)

            def softplus_steps(u, m):
                act.wait_ge(dtraw_done, u + 1)
                nc.scalar.activation(soft[:], p_b[:], ACT.Abs, bias=wdtb[m][:]).then_inc(soft_steps, 1)
                act.wait_ge(soft_steps, 3 * u + 1)
                nc.scalar.activation(soft[:], soft[:], ACT.Exp, scale=-1.0).then_inc(soft_steps, 1)
                act.wait_ge(soft_steps, 3 * u + 2)
                nc.scalar.activation(soft[:], soft[:], ACT.Ln, bias=1.0).then_inc(soft_steps, 1)

            def second_part(u, b):
                act.wait_ge(rest_ready, u + 1)
                nc.scalar.copy(parts[b][64:128, :], rest[64:128, :]).then_inc(part_copied, 1)

            def leave_rows(u, b, unit):
                _, half, image = unit
                rows = slice(CH * half, CH * half + CH)
                act.wait_ge(proj_done, u + 1)
                ge(act, cols_ready, image)
                nc.scalar.copy(rows_out[rows, :, :].rearrange("p w j -> p j w"),
                               p_y[b][rows, :].rearrange("p (j w) -> p j w", w=SIDE)).then_inc(left, 1)

            def decay(u, b, m, s):
                if s == 0:
                    act.wait_ge(dt_ready, u + 1)
                ge(act, scan_done, N * u + s - 3)
                nc.scalar.activation(decays[s % 4][:].rearrange("p (q t) -> p q t", t=SIDE)[:, :, 1:],
                                     dt[b][:, :, 1:], ACT.Exp, scale=wa[m][:, s:s + 1]).then_inc(decay_done, 1)

            def copy_c(u, s):
                act.wait_ge(c_done, N * u + s + 1)
                ge(act, read_done, N * u + s - 3)
                nc.scalar.copy(c_sb[s % 4][:], p_C[s % 2][:]).then_inc(c_copied, 1)

            def slot(u, b, before, unit, after):
                for s in range(N):
                    if s + AHEAD < N:
                        decay(u, b, unit[0], s + AHEAD)
                    elif after:
                        decay(u + 1, 1 - b, after[0], s + AHEAD - N)
                    copy_c(u, s)
                    if s == AT["leave_rows"] and before and before[0] == ROWS:
                        leave_rows(u - 1, 1 - b, before)
                    if s == AT["copy_xi"] and after:
                        copy_xi(u + 1, after[0])
                    if s == AT["silus"] and after:
                        silus(u + 1, 1 - b, after[0])
                        exp_ln_tables()
                    if s == AT["softplus"] and after:
                        first_part(u + 1, 1 - b)
                        softplus_steps(u + 1, after[0])
                    if s == AT["second_part"] and after:
                        second_part(u + 1, 1 - b)

            act.wait_ge(decay_zeroed, 4)
            copy_xi(0, ROWS)
            silus(0, 0, ROWS)
            exp_ln_tables()
            first_part(0, 0)
            softplus_steps(0, ROWS)
            second_part(0, 0)
            for s in range(AHEAD):
                decay(0, 0, ROWS, s)
            each_unit(act, slot)

        @block.gpsimd
        def _(pool):
            def read_state(u, s):
                pool.wait_ge(c_copied, N * u + s + 1)
                ge(pool, y_added, N * u + s - 3)
                pool.wait_ge(scan_done, N * u + s + 1)
                nc.gpsimd.tensor_tensor(read[s % 4][:], state[s % 4][:], c_sb[s % 4][:], ALU.mult).then_inc(read_done, 1)

            def apply_gate(u, b):
                ge(pool, proj_done, u - 1)
                pool.wait_ge(gate_ready, u + 1)
                pool.wait_ge(skip_done, u + 1)
                nc.gpsimd.tensor_tensor(gated[b][:], y_skip[b][:], gate[b][:], ALU.mult).then_inc(gated_done, 1)

            def slot(u, b, before, unit, after):
                for s in range(N):
                    read_state(u, s)
                    if s == AT["gate"] and before:
                        apply_gate(u - 1, 1 - b)

            each_unit(pool, slot)
            apply_gate(UNITS - 1, 1)

        @block.vector
        def _(dve):
            def earlier_taps(u, m):
                acc = p_a[:].rearrange("p (q t) -> p q t", t=SIDE)
                dve.wait_ge(tap0_done, u + 1)
                for k in range(1, TAPS):
                    nc.vector.scalar_tensor_tensor(acc[:, :, k:], xi[:, :, :SIDE - k], wc[m][:, TAPS - 1 - k:TAPS - k],
                                                   acc[:, :, k:], ALU.mult, ALU.add).then_inc(taps_done, 1)
                    if k < TAPS - 1:
                        dve.wait_ge(taps_done, 3 * u + k)

            def relu_and_rest(u, b, m):
                dve.wait_ge(part_copied, 2 * u + 1)
                nc.vector.tensor_tensor(rest[64:128, :], p_a[64:128, :], parts[b][64:128, :],
                                        ALU.subtract).then_inc(rest_ready, 1)
                dve.wait_ge(dtraw_done, u + 1)
                dve.wait_ge(soft_steps, 3 * u + 1)
                nc.vector.tensor_scalar(relu[:], p_b[:], wdtb[m][:], 0.0, ALU.add, ALU.max).then_inc(relu_done, 1)

            def make_dt(u, b):
                dve.wait_ge(soft_steps, 3 * u + 3)
                dve.wait_ge(relu_done, u + 1)
                ge(dve, decay_done, N * (u - 1))
                nc.vector.tensor_tensor(dt[b][:].rearrange("p q t -> p (q t)"), relu[:], soft[:],
                                        ALU.add).then_inc(dt_ready, 1)

            def third_part_and_dtx(u, b):
                dve.wait_ge(part_copied, 2 * u + 2)
                nc.vector.tensor_tensor(parts[b][96:128, :], rest[96:128, :], parts[b][96:128, :],
                                        ALU.subtract).then_inc(parts_ready, 1)
                dve.wait_ge(dt_ready, u + 1)
                ge(dve, drive_done, N * (u - 1))
                nc.vector.tensor_tensor(dtx[b][:], dt[b][:].rearrange("p q t -> p (q t)"), xconv[b][:],
                                        ALU.mult).then_inc(dtx_ready, 1)

            def make_drive(u, b, s):
                if s == 0:
                    dve.wait_ge(dtx_ready, u + 1)
                dve.wait_ge(b_done, N * u + s + 1)
                ge(dve, scan_done, N * u + s - 3)
                nc.vector.tensor_tensor(drive[s % 4][:], dtx[b][:], p_B[s % 2][:], ALU.mult).then_inc(drive_done, 1)

            def scan(u, s):
                dve.wait_ge(decay_done, N * u + s + 1)
                dve.wait_ge(drive_done, N * u + s + 1)
                ge(dve, read_done, N * u + s - 3)
                nc.vector.tensor_tensor_scan(state[s % 4][:], decays[s % 4][:], drive[s % 4][:], 0.0,
                                             ALU.mult, ALU.add).then_inc(scan_done, 1)

            def skip(u, b, m):
                dve.wait_ge(y_added, N * u + N)
                ge(dve, gated_done, u - 1)
                nc.vector.scalar_tensor_tensor(y_skip[b][:], xconv[b][:], wd[m][:], p_y[b][:],
                                               ALU.mult, ALU.add).then_inc(skip_done, 1)

            def leave_cols(u, b, unit):
                _, half, image = unit
                dve.wait_ge(proj_done, u + 1)
                dve.wait_ge(resid_loaded, 16 * image + 16)
                cols = slice(HALF * half, HALF * half + HALF)
                nc.vector.tensor_tensor(result[:, :, cols].rearrange("p j w -> p w j"),
                                        p_y[b][:, 0:256].rearrange("p (w j) -> p w j", w=HALF),
                                        resid[:].rearrange("p (j w) -> p w j", w=SIDE)[:, cols, :],
                                        ALU.add).then_inc(left, 1)

            def hold_rows(image, rows_unit, cols_unit):
                dve.wait_ge(left, rows_unit + 1)
                if cols_unit is not None:
                    dve.wait_ge(xz_done, cols_unit + 1)
                nc.vector.tensor_copy(cols_in[:], rows_out[:]).then_inc(cols_ready, 1)

            def slot(u, b, before, unit, after):
                for s in range(N):
                    if s + 1 < N:
                        make_drive(u, b, s + 1)
                    elif after:
                        make_drive(u + 1, 1 - b, 0)
                    scan(u, s)
                    if s == AT["skip"] and before:
                        skip(u - 1, 1 - b, before[0])
                    if s == AT["hold_rows"] and unit[:2] == (COLS, 1) and not (isinstance(u, int) and u == UNITS - 1):
                        hold_rows(unit[2] + 1, u - 2, u)
                    if s == AT["hold_rows"] and isinstance(u, int) and u == 3:
                        hold_rows(0, 1, None)
                    if s == AT["leave_cols"] and before and before[0] == COLS:
                        leave_cols(u - 1, 1 - b, before)
                    if s == AT["taps"] and after:
                        earlier_taps(u + 1, after[0])
                    if s == AT["relu_and_rest"] and after:
                        relu_and_rest(u + 1, 1 - b, after[0])
                    if s == AT["make_dt"] and after:
                        make_dt(u + 1, 1 - b)
                    if s == AT["dtx"] and after:
                        third_part_and_dtx(u + 1, 1 - b)

            for s in four:
                nc.vector.memset(decays[s][:], 0.0).then_inc(decay_zeroed, 1)
            earlier_taps(0, ROWS)
            relu_and_rest(0, 0, ROWS)
            make_dt(0, 0)
            third_part_and_dtx(0, 0)
            make_drive(0, 0, 0)
            each_unit(dve, slot)
            skip(UNITS - 1, 1, COLS)
            leave_cols(UNITS - 1, 1, (COLS, 1, IMAGES - 1))


def kernel(**inputs):
    import numpy as np
    import concourse.bacc as bacc
    from concourse import mybir as mb
    from concourse.bass_utils import run_bass_kernel_spmd as run

    f32 = mb.dt.float32
    nc = bacc.Bacc("TRN2", target_bir_lowering=False, num_devices=1)
    arrays = {}

    def give(name, a):
        a = np.ascontiguousarray(a)
        arrays[name] = a
        return nc.dram_tensor(name, a.shape, f32, kind="ExternalInput").ap()

    def both(a):
        return np.concatenate([a, a], axis=0)

    x = np.asarray(inputs["x"]).reshape(32, 16, 2, 32, 64).transpose(0, 2, 4, 1, 3).reshape(32, 128, 512)
    wv = np.asarray(inputs["L0_conv_Wv"])
    we = np.asarray(inputs["L0_conv_We"])
    per_parity = []
    for par in range(2):
        main = [we[:, par - out_par + 1] for out_par in range(2)]
        main = np.stack(main, axis=2).transpose(3, 0, 1, 2, 4).reshape(64, 4, 384)
        anti = we[:, 2 if par == 0 else 0].transpose(2, 0, 1, 3).reshape(64, 4, 192)
        per_parity.append(np.concatenate([main, anti], axis=2))
    args = [
        give("in_x", x),
        give("in_wk", both(np.asarray(inputs["L0_conv_Wk"]))),
        give("in_q", np.asarray(inputs["L0_conv_q"]).reshape(32)),
        give("in_wvT", both(wv).T.reshape(2, 16, 128).transpose(1, 0, 2)),
        give("in_wmlp", np.asarray(inputs["L0_conv_Wmlp"]).reshape(2, 16, 4).transpose(1, 0, 2)),
        give("in_alpha", np.asarray(inputs["L0_conv_alpha"]).reshape(1)),
        give("in_we", np.concatenate(per_parity, axis=0)),
        give("in_be", both(np.asarray(inputs["L0_conv_be"]).T)),
    ]
    mamba_w = []
    for m in "td":
        w = {k: np.asarray(inputs[f"L1_conv_{m}_{k}"]) for k in
             ("in_w", "conv_w", "conv_b", "xproj_w", "dt_w", "dt_b", "A_log", "D", "out_w")}
        mamba_w.append({
            "in": give(f"in_{m}_in", w["in_w"].T), "conv": give(f"in_{m}_conv", w["conv_w"]),
            "conv_b": give(f"in_{m}_conv_b", w["conv_b"].reshape(128, 1)),
            "dt_in": give(f"in_{m}_dt_in", w["xproj_w"][0:4]), "dt_out": give(f"in_{m}_dt_out", w["dt_w"].T),
            "bc": give(f"in_{m}_bc", w["xproj_w"][4:36].T), "dt_b": give(f"in_{m}_dt_b", w["dt_b"].reshape(128, 1)),
            "a_log": give(f"in_{m}_a_log", w["A_log"]), "d": give(f"in_{m}_d", w["D"].reshape(128, 1)),
            "out": give(f"in_{m}_out", w["out_w"].T)})
    out = nc.dram_tensor("out_0", (32, 128, 512), f32, kind="ExternalOutput").ap()
    mid_x = nc.dram_tensor("mid_x", (32, 128, 512), f32, kind="Internal").ap()
    mid_n = nc.dram_tensor("mid_n", (32, 128, 512), f32, kind="Internal").ap()
    build(nc, *args, mamba_w, out, mid_x, mid_n)
    got = run(nc, [arrays], core_ids=[0]).results[0]["out_0"]
    return np.ascontiguousarray(
        np.asarray(got).reshape(32, 2, 64, 16, 32).transpose(0, 3, 1, 4, 2).reshape(32, 32, 32, 64))
```

```python
from contextlib import ExitStack

import concourse.bass as bass
from concourse import mybir

IMAGES, SIDE, CH = 32, 32, 64
HEADS, DIM_HEAD, EXPERTS, STEPS = 2, 16, 4, 3
PIX = SIDE * SIDE // 2
ROWS2 = SIDE // 2
INNER, STATES, TAPS = 128, 16, 4
SEQS = PIX // SIDE
UNITS = IMAGES * 4
MAIN, ANTI = 3 * 128, 3 * 64
PHASES = 2 * STEPS


def build(nc, x_in, wk, q, wvT, wmlp, alpha, we, be, mamba_w, out, mid_x, mid_n):
    f32, bf16 = mybir.dt.float32, mybir.dt.bfloat16
    ACT, ALU = mybir.ActivationFunctionType, mybir.AluOpType
    X = mybir.AxisListType.X
    ctx = ExitStack()

    def sb(name, shape, dt=f32):
        return ctx.enter_context(nc.sbuf_tensor(name, shape, dt))

    def sem(name):
        return ctx.enter_context(nc.semaphore(name))

    with ctx:
        ident = sb("ident", [128, 128])
        neg_swap = sb("neg_swap", [128, 128])
        ones = sb("ones", [128, 128])
        group_mean = sb("group_mean", [128, 128])
        same_par = sb("same_par", [128, 128])
        select = sb("select", [128, 2 * STATES, 128], bf16)
        tie = sb("tie", [128, EXPERTS, EXPERTS])
        wk_sb = sb("wk_sb", [128, HEADS * DIM_HEAD])
        q_sb = sb("q_sb", [128, HEADS * DIM_HEAD])
        kq = sb("kq", [128, HEADS])
        score_w = sb("score_w", [128, HEADS, 128])
        wv_sb = sb("wv_sb", [DIM_HEAD, HEADS, 128])
        wmlp_sb = sb("wmlp_sb", [DIM_HEAD, HEADS, EXPERTS])
        route_w = sb("route_w", [128, HEADS, EXPERTS])
        gain = sb("gain", [128, 4])
        we_sb = sb("we_sb", [128, EXPERTS, MAIN + ANTI])
        be_sb = sb("be_sb", [128, EXPERTS])
        wi_rows = sb("wi_rows", [128, 2 * INNER])
        wi_cols = [sb(f"wi_cols{p}", [128, 2 * INNER]) for p in range(2)]
        wc = [sb(f"wc{m}", [128, TAPS]) for m in range(2)]
        wcb = [sb(f"wcb{m}", [128, 1]) for m in range(2)]
        wbc = [sb(f"wbc{m}", [128, 4, 2 * STATES]) for m in range(2)]
        wdt_in = [sb(f"wdt_in{m}", [4, 128]) for m in range(2)]
        wdt_out = [sb(f"wdt_out{m}", [4, 128]) for m in range(2)]
        wdt = [sb(f"wdt{m}", [128, 128]) for m in range(2)]
        wdtb = [sb(f"wdtb{m}", [128, 1]) for m in range(2)]
        wa = [sb(f"wa{m}", [128, STATES]) for m in range(2)]
        wd = [sb(f"wd{m}", [128, 1]) for m in range(2)]
        wo = [sb(f"wo{m}", [128, CH]) for m in range(2)]

        weights_loaded = sem("weights_loaded")
        const_memset = sem("const_memset")
        const_built = sem("const_built")
        kq_ready = sem("kq_ready")
        gain_act = sem("gain_act")
        small_products = sem("small_products")
        a_exp = sem("a_exp")
        dve_chain = sem("dve_chain")

        loads = [(wk_sb[:], wk), (wv_sb[:], wvT), (wmlp_sb[:], wmlp), (we_sb[:], we), (be_sb[:], be),
                 (q_sb[:], q.partition_broadcast(128)), (gain[:, 0:1], alpha.partition_broadcast(128))]
        for m in range(2):
            w = mamba_w[m]
            halves = (wi_rows, wi_rows) if m == 0 else wi_cols
            loads += [(halves[0][0:CH, :], w["in"]), (halves[1][CH:128, :], w["in"]), (wc[m][:], w["conv"]),
                      (wcb[m][:], w["conv_b"]), (wdt_in[m][:], w["dt_in"]), (wdt_out[m][:], w["dt_out"]),
                      (wdtb[m][:], w["dt_b"]), (wa[m][:], w["a_log"]), (wd[m][:], w["d"]), (wo[m][:], w["out"])]
            loads += [(wbc[m][:, r, :], w["bc"]) for r in range(4)]

        with ExitStack() as setup_ctx:
            p_setup = [setup_ctx.enter_context(nc.psum_tensor(f"p_setup{i}", [128, 512], f32)) for i in range(4)]
            block = setup_ctx.enter_context(nc.Block())

            @block.sync
            def _(sp):
                for dst, src in loads:
                    sp.dma_start(dst, src).then_inc(weights_loaded, 16)
                sp.wait_ge(weights_loaded, 16 * len(loads))

            @block.gpsimd
            def _(pool):
                def place(ap, fill, base, pattern, count):
                    nc.gpsimd.affine_select(out=ap, in_=ap, compare_op=ALU.not_equal, fill=fill, base=base,
                                            pattern=pattern, channel_multiplier=1).then_inc(const_built, 1)
                    pool.wait_ge(const_built, count)

                pool.wait_ge(const_memset, 5)
                place(ident[:], 1.0, 0, [[-1, 128]], 1)
                place(neg_swap[:, 0:64], -1.0, -64, [[-1, 64]], 2)
                place(neg_swap[:, 64:128], -1.0, 0, [[-1, 64]], 3)
                n = 3
                for off in (0, 1, 64, 65):
                    n += 1
                    place(group_mean[:].rearrange("p (a g k) -> p a g k", a=2, k=2), 0.25, -off,
                          [[0, 2], [-2, 32], [0, 2]], n)
                for off in (0, 64, 96):
                    n += 1
                    place(select[:], 1.0, -off, [[-1, 2 * STATES], [0, 128]], n)

            @block.vector
            def _(dve):
                nc.vector.memset(wi_cols[0][CH:128, :], 0.0)
                nc.vector.memset(wi_cols[1][0:CH, :], 0.0)
                nc.vector.memset(ident[:], 0.0).then_inc(const_memset, 1)
                nc.vector.memset(neg_swap[:], 0.0).then_inc(const_memset, 1)
                nc.vector.memset(group_mean[:], 0.0).then_inc(const_memset, 1)
                nc.vector.memset(select[:], 0.0).then_inc(const_memset, 1)
                nc.vector.memset(ones[:], 1.0).then_inc(const_memset, 1)
                nc.vector.memset(same_par[:], 0.0).then_inc(dve_chain, 1)
                nc.vector.memset(tie[:], 0.0).then_inc(dve_chain, 1)
                dve.wait_ge(dve_chain, 2)
                nc.vector.memset(same_par[0:64, 0:64], 1.0)
                nc.vector.memset(same_par[64:128, 64:128], 1.0).then_inc(dve_chain, 1)
                for e in range(1, EXPERTS):
                    nc.vector.memset(tie[:, e, 0:e], 1.0).then_inc(dve_chain, 1)
                dve.wait_ge(weights_loaded, 16 * len(loads))
                nc.vector.tensor_tensor(wk_sb[:], wk_sb[:], q_sb[:], ALU.mult).then_inc(dve_chain, 1)
                dve.wait_ge(dve_chain, 7)
                nc.vector.reduce_sum(kq[:], wk_sb[:].rearrange("p (n d) -> p n d", n=HEADS), X).then_inc(dve_chain, 1)
                dve.wait_ge(dve_chain, 8)
                for n in range(HEADS):
                    nc.vector.tensor_scalar(score_w[:, n, :], same_par[:], kq[:, n:n + 1], DIM_HEAD ** -0.5,
                                            ALU.mult, ALU.mult)
                nc.vector.tensor_scalar(gain[:, 2:3], gain[:, 0:1], 0.0, None, ALU.max).then_inc(dve_chain, 1)
                dve.wait_ge(dve_chain, 9)
                dve.wait_ge(gain_act, 3)
                nc.vector.tensor_tensor(gain[:, 3:4], gain[:, 1:2], gain[:, 2:3], ALU.add)
                dve.wait_ge(small_products, 4)
                for n in range(HEADS):
                    nc.vector.tensor_copy(route_w[:, n, :], p_setup[n][:, 0:EXPERTS])
                dve.wait_ge(a_exp, 2)
                for m in range(2):
                    nc.vector.tensor_copy(wdt[m][:], p_setup[2 + m][:, 0:128])
                    nc.vector.tensor_scalar(wa[m][:], wa[m][:], -1.0, None, ALU.mult)

            @block.scalar
            def _(act):
                act.wait_ge(weights_loaded, 16 * len(loads))
                nc.scalar.activation(gain[:, 1:2], gain[:, 0:1], ACT.Abs).then_inc(gain_act, 1)
                act.wait_ge(gain_act, 1)
                nc.scalar.activation(gain[:, 1:2], gain[:, 1:2], ACT.Exp, scale=-1.0).then_inc(gain_act, 1)
                act.wait_ge(gain_act, 2)
                nc.scalar.activation(gain[:, 1:2], gain[:, 1:2], ACT.Ln, bias=1.0).then_inc(gain_act, 1)
                for m in range(2):
                    nc.scalar.activation(wa[m][:], wa[m][:], ACT.Exp).then_inc(a_exp, 1)

            @block.tensor
            def _(pe):
                pe.wait_ge(weights_loaded, 16 * len(loads))
                for n in range(HEADS):
                    nc.tensor.matmul(p_setup[n][:, 0:EXPERTS], wv_sb[:, n, :], wmlp_sb[:, n, :],
                                     start=True, stop=True).then_inc(small_products, 1)
                for m in range(2):
                    nc.tensor.matmul(p_setup[2 + m][:, 0:128], wdt_in[m][:], wdt_out[m][:],
                                     start=True, stop=True).then_inc(small_products, 1)

        stage1(nc, x_in, mid_x, mid_n, dict(
            neg_swap=neg_swap, ones=ones, group_mean=group_mean, tie=tie, score_w=score_w, route_w=route_w,
            gain=gain, we=we_sb, be=be_sb))
        stage2(nc, mid_x, mid_n, out, dict(
            ident=ident, select=select, wi_rows=wi_rows, wi_cols=wi_cols, wc=wc, wcb=wcb,
            wbc=wbc, wdt=wdt, wdtb=wdtb, wa=wa, wd=wd, wo=wo))


def stage1(nc, x_in, mid_x, mid_n, c):
    f32 = mybir.dt.float32
    ACT, ALU = mybir.ActivationFunctionType, mybir.AluOpType
    X = mybir.AxisListType.X
    BODIES = IMAGES // 4
    LINKS = 190
    ctx = ExitStack()
    with ctx:
        def sb(name, shape, dt=f32):
            return ctx.enter_context(nc.sbuf_tensor(name, shape, dt))

        def sem(name):
            return ctx.enter_context(nc.semaphore(name))

        fresh = [[sb(f"fresh_{g}{a}", [128, PIX]) for a in range(2)] for g in range(2)]
        x0 = [[sb(f"x0_{g}{a}", [128, PIX]) for a in range(2)] for g in range(2)]
        xc = [[sb(f"xc_{g}{a}", [128, PIX]) for a in range(2)] for g in range(2)]
        x1 = [[sb(f"x1_{g}{a}", [128, PIX]) for a in range(2)] for g in range(2)]
        xn = [[sb(f"xn_{g}{a}", [128, PIX]) for a in range(2)] for g in range(2)]
        padded = [[sb(f"pad_{g}{a}", [128, ROWS2, SIDE + 2]) for a in range(2)] for g in range(2)]
        shifted = [[sb(f"shf_{g}{a}", [128, ROWS2, SIDE + 2]) for a in range(2)] for g in range(2)]
        w_main = [[sb(f"wm_{g}{a}", [128, 3, 128]) for a in range(2)] for g in range(2)]
        w_anti = [[sb(f"wx_{g}{a}", [128, 3, 128]) for a in range(2)] for g in range(2)]
        mix0 = [sb(f"mix0_{a}", [128, MAIN + ANTI]) for a in range(2)]
        mix1 = [sb(f"mix1_{a}", [128, MAIN + ANTI]) for a in range(2)]
        mix2, mix3 = sb("mix2", [128, MAIN + ANTI]), sb("mix3", [128, MAIN + ANTI])
        attn = [sb(f"attn_{a}", [128, HEADS, PIX]) for a in range(2)]
        modul = [sb(f"modul_{a}", [128, PIX]) for a in range(2)]
        scrap = sb("scrap", [128, HEADS, PIX])
        pool_scrap = sb("pool_scrap", [128, 1])
        pool_scrap2 = sb("pool_scrap2", [128, 1])
        stats = sb("stats", [128, 2, 6])
        moments = sb("moments", [128, 2, 2])
        gn = sb("gn", [128, 10, 2])
        hold = sb("hold", [128, 1])
        top = sb("top", [128, 2, HEADS])
        neg_top = sb("neg_top", [128, 2, HEADS])
        pooled = sb("pooled", [128, 2 * HEADS])
        parts = sb("parts", [128, 2 * HEADS * EXPERTS + 2 * HEADS])
        NP = 2 * HEADS * EXPERTS
        r = sb("r", [128, 2 * HEADS])
        logit_n = sb("logit_n", [128, 2, HEADS, EXPERTS])
        logit = sb("logit", [128, 2, EXPERTS])
        prob = sb("prob", [128, 2, EXPERTS])
        col = sb("col", [128, 6, 2])
        above = sb("above", [128, 2, EXPERTS, EXPERTS])
        equal = sb("equal", [128, 2, EXPERTS, EXPERTS])
        rank = sb("rank", [128, 2, EXPERTS])
        chosen = sb("chosen", [128, 2, EXPERTS])
        wsel = sb("wsel", [128, 2, EXPERTS])
        bias_e = sb("bias_e", [128, 2, EXPERTS])
        bias = [sb(f"bias_{g}", [128, 2]) for g in range(2)]
        allowed = [sb(f"allowed_{g}", [128, 2, EXPERTS]) for g in range(2)]
        penalty = [sb(f"penalty_{g}", [128, 2, EXPERTS]) for g in range(2)]
        kmap = sb("kmap", [128, 2 * HEADS])

        p_score = [ctx.enter_context(nc.psum_tensor(f"p_score{a}", [128, HEADS, 512], f32)) for a in range(2)]
        p_conv = [ctx.enter_context(nc.psum_tensor(f"p_conv{a}", [128, 512], f32)) for a in range(2)]
        p_small = ctx.enter_context(nc.psum_tensor("p_small", [128, 512], f32))
        p_gn = ctx.enter_context(nc.psum_tensor("p_gn", [128, 512], f32))
        P_SWAP, P_SUM, P_MEAN, P_VAR = (slice(0, 4), slice(16, 16 + NP + 4), slice(0, 2), slice(16, 18))

        fresh_x = sem("s1_fresh_x")
        fresh_y = sem("s1_fresh_y")
        loaded_x = sem("s1_loaded_x")
        loaded_y = sem("s1_loaded_y")
        stored_x = sem("s1_stored_x")
        stored_y = sem("s1_stored_y")
        gn_mean_in = sem("s1_gn_mean_in")
        gn_mean = sem("s1_gn_mean")
        gn_var_in = sem("s1_gn_var_in")
        gn_var = sem("s1_gn_var")
        gn_v = sem("s1_gn_v")
        gn_ln = sem("s1_gn_ln")
        gn_rs = sem("s1_gn_rs")
        x_norm = sem("s1_x_norm")
        x_out = sem("s1_x_out")
        x_step = sem("s1_x_step")
        score_done = sem("s1_score_done")
        top_ready = sem("s1_top_ready")
        swap_done = sem("s1_swap_done")
        neg_top_ready = sem("s1_neg_top_ready")
        exp_done = sem("s1_exp_done")
        parts_ready = sem("s1_parts_ready")
        sum_done = sem("s1_sum_done")
        wexp_in = sem("s1_wexp_in")
        wexp_done = sem("s1_wexp_done")
        wsel_ready = sem("s1_wsel_ready")
        scaled = sem("s1_scaled")
        mix_ready = sem("s1_mix_ready")
        mix_paired = sem("s1_mix_paired")
        w_ready = sem("s1_w_ready")
        modul_ready = sem("s1_modul_ready")
        padded_ready = sem("s1_padded_ready")
        shifted_ready = sem("s1_shifted_ready")
        w_main_done, w_even_done = sem("s1_w_main_done"), sem("s1_w_even_done")
        conv_done = sem("s1_conv_done")
        zeroed = sem("s1_zeroed")
        zeroed_dve = sem("s1_zeroed_dve")
        x1_ready = sem("s1_x1_ready")
        link = sem("s1_link")

        block = ctx.enter_context(nc.Block())

        def each_phase(eng, slot):
            for k in range(PHASES - 1):
                slot(0, k, False, True)
            with eng.Fori(0, BODIES - 1) as i:
                slot(i, PHASES - 1, True, True)
                for k in range(PHASES - 1):
                    slot(i + 1, k, True, True)
            slot(BODIES - 1, PHASES - 1, True, False)

        def norm_in_phase(i, k, before, after):
            if k == PHASES - 1:
                return (4 * i + 2, "in", 0) if after else None
            if k == 0:
                return (4 * i - 1 if before else 1, "in", 1)
            if k in (1, 2) and before:
                return (4 * i - 1 + k, "out", k - 1)
            return None

        @block.sync
        def _(sp):
            fetched, done = (loaded_x, loaded_y), (stored_x, stored_y)

            def fetch_fresh(body):
                for g in range(2):
                    for a in range(2):
                        sp.dma_start(fresh[g][a][:], x_in[4 * body + 2 * g + a]).then_inc((fresh_x, fresh_y)[g], 16)

            def fetch(body, g):
                for a in range(2):
                    sp.dma_start(x0[g][a][:], x_in[4 * body + 2 * g + a]).then_inc(fetched[g], 16)

            def store(body, g):
                sp.wait_ge(x_out, 2 * body + g + 1)
                for a in range(2):
                    sp.dma_start(mid_x[4 * body + 2 * g + a], x1[g][a][:]).then_inc(done[g], 16)
                    sp.dma_start(mid_n[4 * body + 2 * g + a], xn[g][a][:]).then_inc(done[g], 16)

            def turn(body):
                for g in range(2):
                    store(body, g)
                    sp.wait_ge(done[g], 64 * body + 64)
                    fetch(body + 1, g)

            fetch_fresh(0)
            for g in range(2):
                fetch(0, g)
            sp.wait_ge(x_norm, 2)
            fetch_fresh(1)
            with sp.Fori(0, BODIES - 2) as i:
                sp.wait_ge(x_norm, 2 * i + 4)
                fetch_fresh(i + 2)
                turn(i)
            turn(BODIES - 2)
            for g in range(2):
                store(BODIES - 1, g)
                sp.wait_ge(done[g], 64 * BODIES)

        @block.tensor
        def _(pe):
            def group_mean(n):
                pe.wait_ge(gn_mean_in, n + 1)
                nc.tensor.matmul(p_gn[:, P_MEAN], c["group_mean"][:], moments[:, :, 0],
                                 start=True, stop=True).then_inc(gn_mean, 1)

            def group_var(n):
                pe.wait_ge(gn_var_in, n + 1)
                nc.tensor.matmul(p_gn[:, P_VAR], c["group_mean"][:], gn[:, 2, :],
                                 start=True, stop=True).then_inc(gn_var, 1)

            def score(i, k):
                g, t = k % 2, k // 2
                for a in range(2):
                    if t == 0:
                        pe.wait_ge(x_norm, 2 * i + g + 1)
                    else:
                        pe.wait_ge(x_step, i * 8 + 2 * (k - 2) + a + 1)
                    for n in range(HEADS):
                        mm = nc.tensor.matmul(p_score[a][:, n, :], c["score_w"][:, n, :], xc[g][a][:],
                                              start=True, stop=True)
                    mm.then_inc(score_done, 1)

            def swap(i, k):
                pe.wait_ge(top_ready, i * PHASES + k + 1)
                nc.tensor.matmul(p_small[:, P_SWAP], c["neg_swap"][:], top[:].rearrange("p a n -> p (a n)"),
                                 start=True, stop=True).then_inc(swap_done, 1)

            def total(i, k):
                pe.wait_ge(parts_ready, i * PHASES + k + 1)
                nc.tensor.matmul(p_small[:, P_SUM], c["ones"][:], parts[:],
                                 start=True, stop=True).then_inc(sum_done, 1)

            def conv_main(i, k, a, before):
                g = k % 2
                P = i * PHASES + k
                pe.wait_ge(w_main_done, 2 * P + a + 1)
                pe.wait_ge(padded_ready, 2 * P + a + 3)
                if 1 <= k <= PHASES - 2:
                    pe.wait_ge(x_step, i * 8 + 2 * (k - 1) + a + 1)
                elif k == PHASES - 1:
                    pe.wait_ge(x1_ready, 4 * i + a + 1)
                elif before:
                    pe.wait_ge(x1_ready, 4 * i - 1 + a)
                for dx in range(3):
                    nc.tensor.matmul(p_conv[a][:], w_main[g][a][:, dx, :], padded[g][a][:, :, dx:dx + SIDE],
                                     start=(dx == 0), stop=False)

            def conv_anti(i, k, a):
                g = k % 2
                P = i * PHASES + k
                pe.wait_ge(w_ready, 2 * P + a + 3)
                pe.wait_ge(shifted_ready, 2 * P + a + 1)
                for dx in range(3):
                    mm = nc.tensor.matmul(p_conv[a][:], w_anti[g][a][:, dx, :], shifted[g][a][:, :, dx:dx + SIDE],
                                          start=False, stop=(dx == 2))
                mm.then_inc(conv_done, 1)

            def slot(i, k, before, after):
                norm = norm_in_phase(i, k, before, after)
                last = (i, k - 1) if k else (i - 1, PHASES - 1)
                last_before = before if k else True
                if k == 0 and before and isinstance(i, int):
                    last_before = i > 1
                runs_conv = k > 0 or before
                if runs_conv:
                    conv_main(*last, 0, last_before)
                swap(i, k)
                if norm:
                    group_mean(norm[0])
                if runs_conv:
                    conv_anti(*last, 0)
                if norm:
                    group_var(norm[0])
                total(i, k)
                if runs_conv:
                    conv_main(*last, 1, last_before)
                    conv_anti(*last, 1)
                if after:
                    score(*((i, k + 1) if k < PHASES - 1 else (i + 1, 0)))

            group_mean(0)
            group_var(0)
            score(0, 0)
            each_phase(pe, slot)
            group_mean(4 * BODIES - 2)
            group_var(4 * BODIES - 2)
            for a in range(2):
                conv_main(BODIES - 1, PHASES - 1, a, True)
                conv_anti(BODIES - 1, PHASES - 1, a)
            group_mean(4 * BODIES - 1)
            group_var(4 * BODIES - 1)

        @block.scalar
        def _(act):
            def group_root(n):
                act.wait_ge(gn_v, n + 1)
                nc.scalar.activation(gn[:, 4, :], gn[:, 3, :], ACT.Ln).then_inc(gn_ln, 1)
                act.wait_ge(gn_ln, n + 1)
                nc.scalar.activation(gn[:, 5, :], gn[:, 4, :], ACT.Exp, scale=-0.5).then_inc(gn_rs, 1)

            def step_out(i, k):
                g = k % 2
                for a in range(2):
                    act.wait_ge(conv_done, (i * PHASES + k) * 2 + a + 1)
                    nc.scalar.activation(xc[g][a][:], p_conv[a][:], ACT.Identity,
                                         bias=bias[g][:, a:a + 1]).then_inc(x_step, 1)

            nc.scalar.preload_act_table_set("natural_log_exp_and_others")
            def slot(i, k, before, after):
                P = i * PHASES + k
                norm = norm_in_phase(i, k, before, after)
                act.wait_ge(neg_top_ready, P + 1)
                for a in range(2):
                    for n in range(HEADS):
                        ex = nc.scalar.activation(attn[a][:, n, :], p_score[a][:, n, :], ACT.Exp,
                                                  bias=neg_top[:, a, n:n + 1],
                                                  accum_out=parts[:, NP + 2 * a + n:NP + 2 * a + n + 1])
                    ex.then_inc(exp_done, 1)
                act.wait_ge(wexp_in, P + 1)
                nc.scalar.activation(prob[:], logit[:], ACT.Exp, scale=1.0 / 1.5).then_inc(wexp_done, 1)
                if norm:
                    group_root(norm[0])
                if 1 <= k <= PHASES - 2:
                    step_out(i, k - 1)
                act.wait_ge(wsel_ready, P + 1)
                for a in range(2):
                    act.wait_ge(w_ready, 2 * P + a + 1)
                    sc = nc.scalar.mul(mix0[a][:], c["we"][:, 0, :], wsel[:, a, 0:1])
                    if a == 0:
                        sc.then_inc(scaled, 1)
                    sc = nc.scalar.mul(mix1[a][:], c["we"][:, 1, :], wsel[:, a, 1:2])
                    if a == 1:
                        nc.scalar.mul(mix2[:], c["we"][:, 2, :], wsel[:, a, 2:3])
                        sc = nc.scalar.mul(mix3[:], c["we"][:, 3, :], wsel[:, a, 3:4])
                    sc.then_inc(scaled, 1)
                    act.wait_ge(padded_ready, 2 * P + a + 3)
                    nc.scalar.copy(shifted[k % 2][a][0:64, 0:ROWS2 - 1, :], padded[k % 2][a][0:64, 1:, :])
                    nc.scalar.copy(shifted[k % 2][a][64:128, 1:ROWS2, :],
                                   padded[k % 2][a][64:128, :ROWS2 - 1, :]).then_inc(shifted_ready, 1)

            nc.scalar.preload_act_table_set("natural_log_exp_and_others")
            group_root(0)
            each_phase(act, slot)
            group_root(4 * BODIES - 2)
            group_root(4 * BODIES - 1)

        @block.gpsimd
        def _(pool):
            for g in range(2):
                for a in range(2):
                    nc.gpsimd.memset(w_anti[g][a][:], 0.0).then_inc(zeroed, 1)
                    nc.gpsimd.memset(shifted[g][a][:], 0.0).then_inc(zeroed, 1)
            pool.wait_ge(zeroed, 8)
            nc.gpsimd.memset(pool_scrap[:], 0.0).then_inc(w_ready, 2)
            nc.gpsimd.memset(pool_scrap2[:], 0.0).then_inc(padded_ready, 2)
            def slot(i, k, before, after):
                g, P = k % 2, i * PHASES + k
                pool.wait_ge(w_ready, 2 * P + 2)
                for a in range(2):
                    pool.wait_ge(modul_ready, 2 * P + a + 1)
                    nc.gpsimd.tensor_tensor(padded[g][a][:, :, 1:SIDE + 1],
                                            modul[a][:].rearrange("p (j w) -> p j w", j=ROWS2),
                                            xc[g][a][:].rearrange("p (j w) -> p j w", j=ROWS2),
                                            ALU.mult).then_inc(padded_ready, 1)
                for a in range(2):
                    if a == 0:
                        pool.wait_ge(mix_ready, P + 1)
                        one, other = mix0[0], mix1[0]
                    else:
                        pool.wait_ge(scaled, 3 * P + 3)
                        nc.gpsimd.tensor_tensor(mix0[1][:], mix0[1][:], mix1[1][:], ALU.add).then_inc(mix_paired, 1)
                        nc.gpsimd.tensor_tensor(mix2[:], mix2[:], mix3[:], ALU.add).then_inc(mix_paired, 1)
                        pool.wait_ge(mix_paired, 2 * P + 2)
                        one, other = mix0[1], mix2
                    nc.gpsimd.tensor_tensor(w_main[g][a][:].rearrange("p d c -> p (d c)"), one[:, 0:MAIN],
                                            other[:, 0:MAIN], ALU.add).then_inc(w_main_done, 1)
                    pool.wait_ge(w_main_done, 2 * P + a + 1)
                    for par in range(2):
                        rows, cols = slice(64 * par, 64 * par + 64), slice(64 - 64 * par, 128 - 64 * par)
                        nc.gpsimd.tensor_tensor(
                            w_anti[g][a][rows, :, cols],
                            one[rows, MAIN:].rearrange("p (d c) -> p d c", d=3),
                            other[rows, MAIN:].rearrange("p (d c) -> p d c", d=3),
                            ALU.add).then_inc((w_even_done, w_ready)[par], 1)
                        if par == 0 or a == 0:
                            pool.wait_ge((w_even_done, w_ready)[par], 2 * P + a + 1 + 2 * par)

            each_phase(pool, slot)

        @block.vector
        def _(dve):
            n_links = [0, 0]

            def linked(ins):
                n_links[0] += 1
                ins.then_inc(link, 1)
                return n_links[0]

            def chain(ins, beside=None):
                mine = linked(ins)
                if beside:
                    beside()
                dve.wait_ge(link, n_links[1] + mine)

            def norm_moments(src):
                for a in range(2):
                    st = nc.vector.bn_stats(stats[:, a, :], src[a][:])
                chain(st)
                nc.vector.memset(hold[:], 0.0)
                for a in range(2):
                    ag = nc.vector.bn_aggr(moments[:, a, :], stats[:, a, :])
                ag.then_inc(gn_mean_in, 1)

            def norm_variance_in(n):
                dve.wait_ge(gn_mean, n + 1)
                chain(nc.vector.tensor_copy(gn[:, 0, :], p_gn[:, P_MEAN]))
                chain(nc.vector.tensor_tensor(gn[:, 1, :], moments[:, :, 0], gn[:, 0, :], ALU.subtract))
                chain(nc.vector.tensor_tensor(gn[:, 2, :], gn[:, 1, :], gn[:, 1, :], ALU.mult))
                nc.vector.tensor_tensor(gn[:, 2, :], gn[:, 2, :], moments[:, :, 1], ALU.add).then_inc(gn_var_in, 1)

            def norm_variance(n):
                dve.wait_ge(gn_var, n + 1)
                nc.vector.tensor_scalar(gn[:, 3, :], p_gn[:, P_VAR], 1e-5, None, ALU.add).then_inc(gn_v, 1)

            def norm_apply(n, src, dst, finish):
                dve.wait_ge(gn_rs, n + 1)
                for src_r, dst_r in ((5, 8), (8, 9)):
                    chain(nc.vector.tensor_tensor(gn[:, 6, :], gn[:, src_r, :], gn[:, src_r, :], ALU.mult))
                    chain(nc.vector.tensor_tensor(gn[:, 6, :], gn[:, 6, :], gn[:, 3, :], ALU.mult))
                    chain(nc.vector.tensor_scalar(gn[:, 6, :], gn[:, 6, :], -0.5, 1.5, ALU.mult, ALU.add))
                    chain(nc.vector.tensor_tensor(gn[:, dst_r, :], gn[:, 6, :], gn[:, src_r, :], ALU.mult))
                for a in range(2):
                    o = nc.vector.tensor_scalar(dst[a][:], src[a][:], gn[:, 0, a:a + 1], gn[:, 9, a:a + 1],
                                                ALU.subtract, ALU.mult)
                o.then_inc(finish, 1)

            def group_norm(n, src, dst, finish):
                norm_moments(src)
                norm_variance_in(n)
                norm_variance(n)
                norm_apply(n, src, dst, finish)

            def step_last(i, g):
                dve.wait_ge((loaded_x, loaded_y)[g], 32 * i + 32)
                k = 2 * (STEPS - 1) + g
                for a in range(2):
                    dve.wait_ge(conv_done, (i * PHASES + k) * 2 + a + 1)
                    o = nc.vector.scalar_tensor_tensor(x1[g][a][:], p_conv[a][:], bias[g][:, a:a + 1], x0[g][a][:],
                                                       ALU.add, ALU.add).then_inc(x1_ready, 1)
                dve.wait_ge(x1_ready, 4 * i + 2 * g + 2)

            def slot(i, k, before, after):
                g, t = k % 2, k // 2
                P = i * PHASES + k
                if k == PHASES - 1 and not isinstance(i, int):
                    in_front = n_links[0] + n_links[1]
                    n_links[0], n_links[1] = 0, i * LINKS + in_front
                    loop_start[0] = in_front
                elif k == PHASES - 1:
                    assert n_links[0] == LINKS, n_links[0]
                    n_links[0], n_links[1] = 0, (BODIES - 1) * LINKS + loop_start[0]
                norm = norm_in_phase(i, k, before, after)
                if norm:
                    number, kind, pair = norm
                    body = i + 1 if k == PHASES - 1 else i
                    src, dst, finish = ((fresh[pair], xc[pair], x_norm) if kind == "in" else
                                        (x1[pair], xn[pair], x_out))
                if t == 0:
                    nc.vector.memset(allowed[g][:], 1.0)
                    chain(nc.vector.memset(penalty[g][:], 0.0))
                for a in range(2):
                    dve.wait_ge(score_done, 2 * P + a + 1)
                    m = nc.vector.reduce_max(top[:, a, :], p_score[a][:], X)
                m.then_inc(top_ready, 1)
                if norm:
                    if kind == "in":
                        dve.wait_ge((fresh_x, fresh_y)[pair], 32 * body + 32)
                    norm_moments(src)
                dve.wait_ge(swap_done, P + 1)
                nc.vector.scalar_tensor_tensor(neg_top[:].rearrange("p a n -> p (a n)"),
                                               top[:].rearrange("p a n -> p (a n)"), -1.0, p_small[:, P_SWAP],
                                               ALU.mult, ALU.min).then_inc(neg_top_ready, 1)
                if 1 <= k <= 2 * (STEPS - 1):
                    chain(nc.vector.scalar_tensor_tensor(allowed[1 - g][:, :, 0:3], rank[:, :, 0:3], 0.5,
                                                         allowed[1 - g][:, :, 0:3], ALU.is_gt, ALU.mult))
                    chain(nc.vector.tensor_scalar(penalty[1 - g][:], allowed[1 - g][:], -1.0, 1e9, ALU.add, ALU.mult))
                if norm:
                    norm_variance_in(number)
                for a in range(2):
                    dve.wait_ge(exp_done, 2 * P + a + 1)
                    for n in range(HEADS):
                        pl = nc.vector.tensor_tensor_reduce(
                            out=scrap[:, n, :], in0=attn[a][:, n, :], in1=xc[g][a][:], scale=1.0, scalar=0.0,
                            op0=ALU.mult, op1=ALU.add, accum_out=pooled[:, 2 * a + n:2 * a + n + 1])
                    chain(pl)
                for a in range(2):
                    pt = nc.vector.tensor_tensor(
                        parts[:, 8 * a:8 * a + 8].rearrange("p (n e) -> p n e", n=HEADS), c["route_w"][:],
                        pooled[:, 2 * a:2 * a + 2].unsqueeze(2).broadcast_to([128, HEADS, EXPERTS]), ALU.mult)
                pt.then_inc(parts_ready, 1)
                dve.wait_ge(sum_done, P + 1)
                chain(nc.vector.reciprocal(r[:], p_small[:, 16 + NP:16 + NP + 4]))
                nc.vector.tensor_scalar(kmap[:], r[:], float(CH * PIX), c["gain"][:, 3:4], ALU.mult, ALU.mult)
                chain(nc.vector.tensor_tensor(
                    logit_n[:].rearrange("p a n e -> p (a n) e"), p_small[:, 16:16 + NP].rearrange("p (m e) -> p m e", e=4),
                    r[:].unsqueeze(2).broadcast_to([128, 4, EXPERTS]), ALU.mult))

                def modulate_0(a):
                    dve.wait_ge(padded_ready, 2 * P + a + 1)
                    linked(nc.vector.tensor_scalar(modul[a][:], attn[a][:, 0, :], kmap[:, 2 * a:2 * a + 1], 1.0,
                                                   ALU.mult, ALU.add))

                def modulate_1(a):
                    nc.vector.scalar_tensor_tensor(modul[a][:], attn[a][:, 1, :], kmap[:, 2 * a + 1:2 * a + 2],
                                                   modul[a][:], ALU.mult, ALU.add).then_inc(modul_ready, 1)

                chain(nc.vector.tensor_tensor(logit[:], logit_n[:, :, 0, :], logit_n[:, :, 1, :], ALU.add),
                      lambda: modulate_0(0))
                chain(nc.vector.scalar_tensor_tensor(logit[:], logit[:], float(CH), allowed[g][:], ALU.mult, ALU.mult),
                      lambda: modulate_0(1))
                chain(nc.vector.tensor_tensor(logit[:], logit[:], penalty[g][:], ALU.add),
                      lambda: modulate_1(0))
                chain(nc.vector.reduce_max(col[:, 0, :], logit[:], X))

                def per_image(j):
                    return col[:, j, :].unsqueeze(2).broadcast_to([128, 2, EXPERTS])

                nc.vector.tensor_tensor(logit[:], logit[:], per_image(0), ALU.subtract).then_inc(wexp_in, 1)
                if norm:
                    norm_variance(number)
                dve.wait_ge(wexp_done, P + 1)
                chain(nc.vector.reduce_sum(col[:, 1, :], prob[:], X))
                chain(nc.vector.reciprocal(col[:, 2, :], col[:, 1, :]))
                chain(nc.vector.tensor_tensor(prob[:], prob[:], per_image(2), ALU.mult))
                w_e = prob[:].unsqueeze(3).broadcast_to([128, 2, EXPERTS, EXPERTS])
                w_j = prob[:].unsqueeze(2).broadcast_to([128, 2, EXPERTS, EXPERTS])
                nc.vector.tensor_tensor(above[:], w_j, w_e, ALU.is_gt)
                chain(nc.vector.tensor_tensor(equal[:], w_j, w_e, ALU.is_equal))
                chain(nc.vector.tensor_tensor(equal[:], equal[:],
                                              c["tie"][:].unsqueeze(1).broadcast_to([128, 2, EXPERTS, EXPERTS]), ALU.mult))
                chain(nc.vector.tensor_tensor(above[:], above[:], equal[:], ALU.add))
                chain(nc.vector.reduce_sum(rank[:], above[:], X))
                chain(nc.vector.scalar_tensor_tensor(chosen[:], rank[:], 1.5, prob[:], ALU.is_lt, ALU.mult))
                chain(nc.vector.reduce_sum(col[:, 3, :], chosen[:], X))
                chain(nc.vector.tensor_scalar(col[:, 4, :], col[:, 3, :], 1e-9, None, ALU.add))
                chain(nc.vector.reciprocal(col[:, 5, :], col[:, 4, :]))
                nc.vector.tensor_tensor(wsel[:], chosen[:], per_image(5), ALU.mult).then_inc(wsel_ready, 1)
                modulate_1(1)
                if norm and kind == "in":
                    dve.wait_ge(padded_ready, 2 * P + 2)
                    norm_apply(number, src, dst, finish)
                dve.wait_ge(wsel_ready, P + 1)
                chain(nc.vector.tensor_tensor(bias_e[:], wsel[:],
                                              c["be"][:].unsqueeze(1).broadcast_to([128, 2, EXPERTS]), ALU.mult))
                nc.vector.reduce_sum(bias[g][:], bias_e[:], X)

                if k == PHASES - 1:
                    step_last(i, 0)
                elif k == 0 and before:
                    step_last(i - 1, 1)
                dve.wait_ge(scaled, 3 * P + 1)
                nc.vector.scalar_tensor_tensor(mix0[0][:], c["we"][:, 2, :], wsel[:, 0, 2:3], mix0[0][:],
                                               ALU.mult, ALU.add)
                dve.wait_ge(scaled, 3 * P + 2)
                nc.vector.scalar_tensor_tensor(mix1[0][:], c["we"][:, 3, :], wsel[:, 0, 3:4], mix1[0][:],
                                               ALU.mult, ALU.add).then_inc(mix_ready, 1)
                if norm and kind == "out":
                    norm_apply(number, src, dst, finish)

            loop_start = [0]
            for g in range(2):
                for a in range(2):
                    nc.vector.memset(padded[g][a][:], 0.0).then_inc(zeroed_dve, 1)
            dve.wait_ge(zeroed_dve, 4)
            dve.wait_ge(fresh_x, 32)
            group_norm(0, fresh[0], xc[0], x_norm)
            each_phase(dve, slot)
            group_norm(4 * BODIES - 2, x1[0], xn[0], x_out)
            step_last(BODIES - 1, 1)
            group_norm(4 * BODIES - 1, x1[1], xn[1], x_out)


def stage2(nc, mid_x, mid_n, out, c):
    f32, bf16 = mybir.dt.float32, mybir.dt.bfloat16
    ACT, ALU = mybir.ActivationFunctionType, mybir.AluOpType
    ident, select, wi_rows, wi_cols, wc, wcb, wbc, wdt, wdtb, wa, wd, wo = (
        c[k] for k in ("ident", "select", "wi_rows", "wi_cols", "wc", "wcb", "wbc", "wdt", "wdtb", "wa", "wd", "wo"))
    N = STATES
    HALF = SIDE // 2
    ROWS, COLS = 0, 1
    BODIES = IMAGES - 2
    DEEP = 8
    LAG = 4
    AHEAD = 2
    AT = dict(skip=3, gate=3, project_out=8, leave_rows=8, leave_cols=7,
              project_in=0, copy_xi=1, current_tap=2, taps=3, project_z=3, silus=6,
              project_bc=8, project_dt=8, first_part=8, rest=9, second_part=10, soft=10, relu=10,
              third_part=12, make_dt=12, dtx=12)

    ctx = ExitStack()
    with ctx:
        def sb(name, shape, dt=f32):
            return ctx.enter_context(nc.sbuf_tensor(name, shape, dt))

        def ps(name):
            return ctx.enter_context(nc.psum_tensor(name, [128, 512], f32))

        def sem(name):
            return ctx.enter_context(nc.semaphore(name))

        norm_in = sb("norm_in", [128, PIX])
        resid = sb("resid", [128, PIX])
        rows_out = sb("rows_out", [128, SIDE, ROWS2])
        cols_in = sb("cols_in", [128, SIDE, ROWS2])
        result = sb("result", [128, ROWS2, SIDE])
        two, four = range(2), range(4)
        xi = sb("xi", [128, SEQS, SIDE])
        gate = [sb(f"gate{b}", [128, PIX]) for b in two]
        xconv = [sb(f"xconv{b}", [128, PIX]) for b in two]
        soft = sb("soft", [128, PIX])
        relu = sb("relu", [128, PIX])
        dt = [sb(f"dt{b}", [128, SEQS, SIDE]) for b in two]
        dtx = [sb(f"dtx{b}", [128, PIX]) for b in two]
        parts = [sb(f"bcparts{b}", [128, PIX], bf16) for b in two]
        rest = sb("rest", [128, PIX])
        drive = [sb(f"drive{b}", [128, PIX]) for b in four]
        decays = [sb(f"decays{b}", [128, PIX]) for b in range(DEEP)]
        state = [sb(f"state{b}", [128, PIX]) for b in four]
        c_sb = [sb(f"c_sb{b}", [128, PIX]) for b in range(DEEP)]
        read = [sb(f"read{b}", [128, PIX]) for b in four]
        y_skip = [sb(f"y_skip{b}", [128, PIX]) for b in two]
        gated = [sb(f"gated{b}", [128, PIX]) for b in two]

        p_a, p_b = ps("p_a"), ps("p_b")
        p_B = [ps("p_B0"), ps("p_B1")]
        p_C = [ps("p_C0"), ps("p_C1")]
        p_y = [ps("p_y0"), ps("p_y1")]

        norm_loaded = sem("norm_loaded")
        resid_loaded = sem("resid_loaded")
        out_stored = sem("out_stored")
        xi_done = sem("xi_done")
        z_done = sem("z_done")
        xi_copied = sem("xi_copied")
        tap0_done = sem("tap0_done")
        taps_done = sem("taps_done")
        gate_ready = sem("gate_ready")
        xconv_ready = sem("xconv_ready")
        dtraw_done = sem("dtraw_done")
        bc_done = sem("bc_done")
        soft_steps = sem("soft_steps")
        relu_done = sem("relu_done")
        dt_ready = sem("dt_ready")
        dtx_ready = sem("dtx_ready")
        part_copied = sem("part_copied")
        rest_ready = sem("rest_ready")
        parts_ready = sem("parts_ready")
        b_done = sem("b_done")
        c_done = sem("c_done")
        c_copied = sem("c_copied")
        decay_done = sem("decay_done")
        drive_done = sem("drive_done")
        scan_done = sem("scan_done")
        read_done = sem("read_done")
        y_added = sem("y_added")
        skip_done = sem("skip_done")
        gated_done = sem("gated_done")
        proj_done = sem("proj_done")
        left = sem("left")
        cols_ready = sem("cols_ready")
        decay_zeroed = sem("decay_zeroed")

        def ge(eng, s, value):
            if not isinstance(value, int) or value > 0:
                eng.wait_ge(s, value)

        def each_unit(eng, slot):
            first = [(ROWS, v % 2, v // 2) for v in range(4)]
            last = [(COLS, v % 2, IMAGES - 2 + v // 2) for v in range(4)]

            def around(i):
                return [(ROWS, 1, i + 1), (COLS, 0, i), (COLS, 1, i), (ROWS, 0, i + 2), (ROWS, 1, i + 2),
                        (COLS, 0, i + 1)]

            for v in range(4):
                slot(v, v % 2, first[v - 1] if v else None, first[v], (first + [(COLS, 0, 0)])[v + 1])
            with eng.Fori(0, BODIES) as i:
                units = around(i)
                for v in range(4):
                    slot(4 + 4 * i + v, v % 2, units[v], units[v + 1], units[v + 2])
            for v in range(4):
                slot(UNITS - 4 + v, v % 2, last[v - 1] if v else (ROWS, 1, IMAGES - 1), last[v],
                     last[v + 1] if v < 3 else None)

        block = ctx.enter_context(nc.Block())

        @block.sync
        def _(sp):
            sp.dma_start(norm_in[:], mid_n[0]).then_inc(norm_loaded, 16)
            sp.dma_start(resid[:], mid_x[0]).then_inc(resid_loaded, 16)
            for n in (1, 2):
                sp.wait_ge(z_done, 2 * n)
                sp.dma_start(norm_in[:], mid_n[n]).then_inc(norm_loaded, 16)
            with sp.Fori(0, BODIES - 1) as i:
                sp.wait_ge(left, 4 * i + 6)
                sp.dma_start(out[i], result[:].rearrange("p j w -> p (j w)")).then_inc(out_stored, 16)
                sp.wait_ge(z_done, 4 * i + 8)
                sp.dma_start(norm_in[:], mid_n[i + 3]).then_inc(norm_loaded, 16)
                sp.wait_ge(out_stored, 16 * i + 16)
                sp.dma_start(resid[:], mid_x[i + 1]).then_inc(resid_loaded, 16)
            for n in range(BODIES - 1, IMAGES):
                sp.wait_ge(left, 4 * n + 6 if n < IMAGES - 1 else UNITS)
                sp.dma_start(out[n], result[:].rearrange("p j w -> p (j w)")).then_inc(out_stored, 16)
                sp.wait_ge(out_stored, 16 * (n + 1))
                if n < IMAGES - 1:
                    sp.dma_start(resid[:], mid_x[n + 1]).then_inc(resid_loaded, 16)

        @block.tensor
        def _(pe):
            def project_in(u, unit, z):
                m, half, image = unit
                bank = (p_a, p_b)[z]
                columns = slice(INNER * z, INNER * z + INNER)
                done = (xi_done, z_done)[z]
                if z:
                    ge(pe, relu_done, u)
                    ge(pe, soft_steps, 3 * u - 2)
                elif m == ROWS:
                    pe.wait_ge(norm_loaded, 16 * image + 16)
                else:
                    pe.wait_ge(cols_ready, image + 1)
                if not z:
                    ge(pe, rest_ready, u)
                if m == ROWS:
                    par = slice(CH * half, CH * half + CH)
                    nc.tensor.matmul(bank[:], wi_rows[par, columns], norm_in[par, :],
                                     start=True, stop=True).then_inc(done, 1)
                else:
                    for p in two:
                        mm = nc.tensor.matmul(bank[:, 256 * p:256 * p + 256], wi_cols[p][:, columns],
                                              cols_in[:, HALF * half:HALF * half + HALF, :], start=True, stop=True)
                    mm.then_inc(done, 1)

            def project_bc(u, b, unit):
                m = unit[0]
                pe.wait_ge(xconv_ready, u + 1)
                nc.tensor.matmul(p_a[:], wbc[m][:].rearrange("p a n -> p (a n)"), xconv[b][:],
                                 start=True, stop=True).then_inc(bc_done, 1)

            def project_dt(u, b, unit):
                m = unit[0]
                pe.wait_ge(xconv_ready, u + 1)
                pe.wait_ge(gate_ready, u + 1)
                nc.tensor.matmul(p_b[:], wdt[m][:], xconv[b][:], start=True, stop=True).then_inc(dtraw_done, 1)

            def spread_b(u, b, s):
                if s == 0:
                    pe.wait_ge(parts_ready, u + 1)
                ge(pe, drive_done, N * u + s - 1)
                nc.tensor.matmul(p_B[s % 2][:], select[:, s, :], parts[b][:], start=True, stop=True).then_inc(b_done, 1)

            def spread_c(u, b, s):
                ge(pe, c_copied, N * u + s - 1)
                nc.tensor.matmul(p_C[s % 2][:], select[:, N + s, :], parts[b][:], start=True, stop=True).then_inc(c_done, 1)

            def add_state(u, b, s):
                if s == 0:
                    ge(pe, left, u - 1)
                pe.wait_ge(read_done, N * u + s + 1)
                nc.tensor.matmul(p_y[b][:], ident[:], read[s % 4][:], start=(s == 0), stop=(s == N - 1)).then_inc(y_added, 1)

            def project_out(u, b, unit):
                m, half, _ = unit
                pe.wait_ge(gated_done, u + 1)
                if m == ROWS:
                    mm = nc.tensor.matmul(p_y[b][CH * half:CH * half + CH, :], wo[0][:], gated[b][:],
                                          start=True, stop=True)
                else:
                    by_parity = gated[b][:].rearrange("p (n r) -> p n r", r=2)
                    for p in two:
                        mm = nc.tensor.matmul(p_y[b][CH * p:CH * p + CH, 0:256], wo[1][:], by_parity[:, :, p],
                                              start=True, stop=True)
                mm.then_inc(proj_done, 1)

            def slot(u, b, before, unit, after):
                for s in range(N):
                    if s + 1 < N:
                        spread_b(u, b, s + 1)
                    elif after:
                        spread_b(u + 1, 1 - b, 0)
                    spread_c(u, b, s)
                    if s >= LAG:
                        add_state(u, b, s - LAG)
                    elif before:
                        add_state(u - 1, 1 - b, N - LAG + s)
                    if s == AT["project_out"] and before:
                        project_out(u - 1, 1 - b, before)
                    if s == AT["project_in"] and after:
                        project_in(u + 1, after, 0)
                    if s == AT["project_z"] and after:
                        project_in(u + 1, after, 1)
                    if s == AT["project_bc"] and after:
                        project_bc(u + 1, 1 - b, after)
                    if s == AT["project_dt"] and after:
                        project_dt(u + 1, 1 - b, after)

            project_in(0, (ROWS, 0, 0), 0)
            project_in(0, (ROWS, 0, 0), 1)
            project_bc(0, 0, (ROWS, 0, 0))
            project_dt(0, 0, (ROWS, 0, 0))
            spread_b(0, 0, 0)
            each_unit(pe, slot)
            for s in range(N - LAG, N):
                add_state(UNITS - 1, 1, s)
            project_out(UNITS - 1, 1, (COLS, 1, IMAGES - 1))

        @block.scalar
        def _(act):
            def in_order(bank, m):
                if m == ROWS:
                    return bank[:].rearrange("p (q t) -> p q t", t=SIDE)
                return bank[:].rearrange("p (r w j) -> p w j r", r=2, w=HALF)

            def same_shape(ap, m):
                if m == ROWS:
                    return ap.rearrange("p (q t) -> p q t", t=SIDE)
                return ap.rearrange("p (w j r) -> p w j r", w=HALF, r=2)

            def copy_xi(u, m):
                act.wait_ge(xi_done, u + 1)
                nc.scalar.copy(same_shape(xi[:].rearrange("p q t -> p (q t)"), m), in_order(p_a, m)).then_inc(xi_copied, 1)

            def current_tap(u, m):
                act.wait_ge(xi_copied, u + 1)
                nc.scalar.activation(p_a[:], xi[:].rearrange("p q t -> p (q t)"), ACT.Identity,
                                     bias=wcb[m][:], scale=wc[m][:, TAPS - 1:TAPS]).then_inc(tap0_done, 1)

            def silus(u, b, m):
                act.wait_ge(z_done, u + 1)
                ge(act, gated_done, u - 1)
                nc.scalar.activation(same_shape(gate[b][:], m), in_order(p_b, m), ACT.Silu).then_inc(gate_ready, 1)
                act.wait_ge(taps_done, 3 * u + 3)
                ge(act, skip_done, u - 1)
                nc.scalar.activation(xconv[b][:], p_a[:], ACT.Silu).then_inc(xconv_ready, 1)

            def exp_ln_tables():
                nc.scalar.preload_act_table_set("natural_log_exp_and_others")

            def first_part(u, b):
                act.wait_ge(bc_done, u + 1)
                ge(act, c_done, N * (u - 1))
                nc.scalar.copy(parts[b][:], p_a[:]).then_inc(part_copied, 1)

            def soft_step(u, m, k):
                if k == 0:
                    act.wait_ge(dtraw_done, u + 1)
                    nc.scalar.activation(soft[:], p_b[:], ACT.Abs, bias=wdtb[m][:]).then_inc(soft_steps, 1)
                elif k == 1:
                    act.wait_ge(soft_steps, 3 * u + 1)
                    nc.scalar.activation(soft[:], soft[:], ACT.Exp, scale=-1.0).then_inc(soft_steps, 1)
                else:
                    act.wait_ge(soft_steps, 3 * u + 2)
                    nc.scalar.activation(soft[:], soft[:], ACT.Ln, bias=1.0).then_inc(soft_steps, 1)

            def second_part(u, b):
                act.wait_ge(rest_ready, u + 1)
                nc.scalar.copy(parts[b][64:128, :], rest[64:128, :]).then_inc(part_copied, 1)

            def leave_rows(u, b, unit):
                _, half, image = unit
                rows = slice(CH * half, CH * half + CH)
                act.wait_ge(proj_done, u + 1)
                ge(act, cols_ready, image)
                nc.scalar.copy(rows_out[rows, :, :].rearrange("p w j -> p j w"),
                               p_y[b][rows, :].rearrange("p (j w) -> p j w", w=SIDE)).then_inc(left, 1)

            def decay(u, b, m, s):
                if s == 0:
                    act.wait_ge(dt_ready, u + 1)
                ge(act, scan_done, N * u + s + 1 - DEEP)
                nc.scalar.activation(decays[s % DEEP][:].rearrange("p (q t) -> p q t", t=SIDE)[:, :, 1:],
                                     dt[b][:, :, 1:], ACT.Exp, scale=wa[m][:, s:s + 1]).then_inc(decay_done, 1)

            def copy_c(u, s):
                act.wait_ge(c_done, N * u + s + 1)
                ge(act, read_done, N * u + s + 1 - DEEP)
                nc.scalar.copy(c_sb[s % DEEP][:], p_C[s % 2][:]).then_inc(c_copied, 1)

            def slot(u, b, before, unit, after):
                for s in range(N):
                    if s + AHEAD < N:
                        decay(u, b, unit[0], s + AHEAD)
                    elif after:
                        decay(u + 1, 1 - b, after[0], s + AHEAD - N)
                    copy_c(u, s)
                    if s == AT["leave_rows"] and before and before[0] == ROWS:
                        leave_rows(u - 1, 1 - b, before)
                    if s == AT["copy_xi"] and after:
                        copy_xi(u + 1, after[0])
                    if s == AT["current_tap"] and after:
                        current_tap(u + 1, after[0])
                    if s == AT["silus"] and after:
                        silus(u + 1, 1 - b, after[0])
                        exp_ln_tables()
                    if s == AT["first_part"] and after:
                        first_part(u + 1, 1 - b)
                    if AT["soft"] <= s < AT["soft"] + 3 and after:
                        soft_step(u + 1, after[0], s - AT["soft"])
                    if s == AT["second_part"] and after:
                        second_part(u + 1, 1 - b)

            act.wait_ge(decay_zeroed, DEEP)
            copy_xi(0, ROWS)
            current_tap(0, ROWS)
            silus(0, 0, ROWS)
            exp_ln_tables()
            first_part(0, 0)
            for k in range(3):
                soft_step(0, ROWS, k)
            second_part(0, 0)
            for s in range(AHEAD):
                decay(0, 0, ROWS, s)
            each_unit(act, slot)

        @block.gpsimd
        def _(pool):
            def read_state(u, s):
                pool.wait_ge(c_copied, N * u + s + 1)
                ge(pool, y_added, N * u + s - 3)
                pool.wait_ge(scan_done, N * u + s + 1)
                nc.gpsimd.tensor_tensor(read[s % 4][:], state[s % 4][:], c_sb[s % DEEP][:], ALU.mult).then_inc(read_done, 1)

            def make_dtx(u, b):
                pool.wait_ge(dt_ready, u + 1)
                ge(pool, drive_done, N * (u - 1))
                nc.gpsimd.tensor_tensor(dtx[b][:], dt[b][:].rearrange("p q t -> p (q t)"), xconv[b][:],
                                        ALU.mult).then_inc(dtx_ready, 1)

            def apply_gate(u, b):
                ge(pool, proj_done, u - 1)
                pool.wait_ge(gate_ready, u + 1)
                pool.wait_ge(skip_done, u + 1)
                nc.gpsimd.tensor_tensor(gated[b][:], y_skip[b][:], gate[b][:], ALU.mult).then_inc(gated_done, 1)

            def slot(u, b, before, unit, after):
                for s in range(N):
                    read_state(u, s)
                    if s == AT["gate"] and before:
                        apply_gate(u - 1, 1 - b)
                    if s == AT["dtx"] and after:
                        make_dtx(u + 1, 1 - b)

            make_dtx(0, 0)
            each_unit(pool, slot)
            apply_gate(UNITS - 1, 1)

        @block.vector
        def _(dve):
            def earlier_tap(u, m, k):
                acc = p_a[:].rearrange("p (q t) -> p q t", t=SIDE)
                if k == 1:
                    dve.wait_ge(tap0_done, u + 1)
                else:
                    dve.wait_ge(taps_done, 3 * u + k - 1)
                nc.vector.scalar_tensor_tensor(acc[:, :, k:], xi[:, :, :SIDE - k], wc[m][:, TAPS - 1 - k:TAPS - k],
                                               acc[:, :, k:], ALU.mult, ALU.add).then_inc(taps_done, 1)

            def first_rest(u, b):
                dve.wait_ge(part_copied, 2 * u + 1)
                nc.vector.tensor_tensor(rest[64:128, :], p_a[64:128, :], parts[b][64:128, :],
                                        ALU.subtract).then_inc(rest_ready, 1)

            def make_relu(u, m):
                dve.wait_ge(dtraw_done, u + 1)
                dve.wait_ge(soft_steps, 3 * u + 1)
                nc.vector.tensor_scalar(relu[:], p_b[:], wdtb[m][:], 0.0, ALU.add, ALU.max).then_inc(relu_done, 1)

            def make_dt(u, b):
                dve.wait_ge(soft_steps, 3 * u + 3)
                dve.wait_ge(relu_done, u + 1)
                ge(dve, decay_done, N * (u - 1))
                nc.vector.tensor_tensor(dt[b][:].rearrange("p q t -> p (q t)"), relu[:], soft[:],
                                        ALU.add).then_inc(dt_ready, 1)

            def third_part(u, b):
                dve.wait_ge(part_copied, 2 * u + 2)
                nc.vector.tensor_tensor(parts[b][96:128, :], rest[96:128, :], parts[b][96:128, :],
                                        ALU.subtract).then_inc(parts_ready, 1)

            def make_drive(u, b, s):
                if s == 0:
                    dve.wait_ge(dtx_ready, u + 1)
                dve.wait_ge(b_done, N * u + s + 1)
                ge(dve, scan_done, N * u + s - 3)
                nc.vector.tensor_tensor(drive[s % 4][:], dtx[b][:], p_B[s % 2][:], ALU.mult).then_inc(drive_done, 1)

            def scan(u, s):
                dve.wait_ge(decay_done, N * u + s + 1)
                dve.wait_ge(drive_done, N * u + s + 1)
                ge(dve, read_done, N * u + s - 3)
                nc.vector.tensor_tensor_scan(state[s % 4][:], decays[s % DEEP][:], drive[s % 4][:], 0.0,
                                             ALU.mult, ALU.add).then_inc(scan_done, 1)

            def skip(u, b, m):
                dve.wait_ge(y_added, N * u + N)
                ge(dve, gated_done, u - 1)
                nc.vector.scalar_tensor_tensor(y_skip[b][:], xconv[b][:], wd[m][:], p_y[b][:],
                                               ALU.mult, ALU.add).then_inc(skip_done, 1)

            def leave_cols(u, b, unit):
                _, half, image = unit
                dve.wait_ge(proj_done, u + 1)
                dve.wait_ge(resid_loaded, 16 * image + 16)
                cols = slice(HALF * half, HALF * half + HALF)
                nc.vector.tensor_tensor(result[:, :, cols].rearrange("p j w -> p w j"),
                                        p_y[b][:, 0:256].rearrange("p (w j) -> p w j", w=HALF),
                                        resid[:].rearrange("p (j w) -> p w j", w=SIDE)[:, cols, :],
                                        ALU.add).then_inc(left, 1)

            def hold_rows(image, rows_unit, cols_unit):
                dve.wait_ge(left, rows_unit + 1)
                if cols_unit is not None:
                    dve.wait_ge(z_done, cols_unit + 1)
                nc.vector.tensor_copy(cols_in[:], rows_out[:]).then_inc(cols_ready, 1)

            def slot(u, b, before, unit, after):
                if unit[:2] == (COLS, 1) and not (isinstance(u, int) and u == UNITS - 1):
                    hold_rows(unit[2] + 1, u - 2, u)
                if isinstance(u, int) and u == 3:
                    hold_rows(0, 1, None)
                for s in range(N):
                    if s + 1 < N:
                        make_drive(u, b, s + 1)
                    elif after:
                        make_drive(u + 1, 1 - b, 0)
                    scan(u, s)
                    if s == AT["skip"] and before:
                        skip(u - 1, 1 - b, before[0])
                    if s == AT["leave_cols"] and before and before[0] == COLS:
                        leave_cols(u - 1, 1 - b, before)
                    if AT["taps"] <= s < AT["taps"] + 3 and after:
                        earlier_tap(u + 1, after[0], s - AT["taps"] + 1)
                    if s == AT["rest"] and after:
                        first_rest(u + 1, 1 - b)
                    if s == AT["relu"] and after:
                        make_relu(u + 1, after[0])
                    if s == AT["third_part"] and after:
                        third_part(u + 1, 1 - b)
                    if s == AT["make_dt"] and after:
                        make_dt(u + 1, 1 - b)

            for s in range(DEEP):
                nc.vector.memset(decays[s][:], 0.0).then_inc(decay_zeroed, 1)
            for k in range(1, TAPS):
                earlier_tap(0, ROWS, k)
            first_rest(0, 0)
            make_relu(0, ROWS)
            third_part(0, 0)
            make_dt(0, 0)
            make_drive(0, 0, 0)
            each_unit(dve, slot)
            skip(UNITS - 1, 1, COLS)
            leave_cols(UNITS - 1, 1, (COLS, 1, IMAGES - 1))


def kernel(**inputs):
    import numpy as np
    import concourse.bacc as bacc
    from concourse import mybir as mb
    from concourse.bass_utils import run_bass_kernel_spmd as run

    f32 = mb.dt.float32
    nc = bacc.Bacc("TRN2", target_bir_lowering=False, num_devices=1)
    arrays = {}

    def give(name, a):
        a = np.ascontiguousarray(a)
        arrays[name] = a
        return nc.dram_tensor(name, a.shape, f32, kind="ExternalInput").ap()

    def both(a):
        return np.concatenate([a, a], axis=0)

    x = np.asarray(inputs["x"]).reshape(32, 16, 2, 32, 64).transpose(0, 2, 4, 1, 3).reshape(32, 128, 512)
    wv = np.asarray(inputs["L0_conv_Wv"])
    we = np.asarray(inputs["L0_conv_We"])
    per_parity = []
    for par in range(2):
        main = [we[:, par - out_par + 1] for out_par in range(2)]
        main = np.stack(main, axis=2).transpose(3, 0, 1, 2, 4).reshape(64, 4, 384)
        anti = we[:, 2 if par == 0 else 0].transpose(2, 0, 1, 3).reshape(64, 4, 192)
        per_parity.append(np.concatenate([main, anti], axis=2))
    args = [
        give("in_x", x),
        give("in_wk", both(np.asarray(inputs["L0_conv_Wk"]))),
        give("in_q", np.asarray(inputs["L0_conv_q"]).reshape(32)),
        give("in_wvT", both(wv).T.reshape(2, 16, 128).transpose(1, 0, 2)),
        give("in_wmlp", np.asarray(inputs["L0_conv_Wmlp"]).reshape(2, 16, 4).transpose(1, 0, 2)),
        give("in_alpha", np.asarray(inputs["L0_conv_alpha"]).reshape(1)),
        give("in_we", np.concatenate(per_parity, axis=0)),
        give("in_be", both(np.asarray(inputs["L0_conv_be"]).T)),
    ]
    mamba_w = []
    for m in "td":
        w = {k: np.asarray(inputs[f"L1_conv_{m}_{k}"]) for k in
             ("in_w", "conv_w", "conv_b", "xproj_w", "dt_w", "dt_b", "A_log", "D", "out_w")}
        mamba_w.append({
            "in": give(f"in_{m}_in", w["in_w"].T), "conv": give(f"in_{m}_conv", w["conv_w"]),
            "conv_b": give(f"in_{m}_conv_b", w["conv_b"].reshape(128, 1)),
            "dt_in": give(f"in_{m}_dt_in", w["xproj_w"][0:4]), "dt_out": give(f"in_{m}_dt_out", w["dt_w"].T),
            "bc": give(f"in_{m}_bc", w["xproj_w"][4:36].T), "dt_b": give(f"in_{m}_dt_b", w["dt_b"].reshape(128, 1)),
            "a_log": give(f"in_{m}_a_log", w["A_log"]), "d": give(f"in_{m}_d", w["D"].reshape(128, 1)),
            "out": give(f"in_{m}_out", w["out_w"].T)})
    out = nc.dram_tensor("out_0", (32, 128, 512), f32, kind="ExternalOutput").ap()
    mid_x = nc.dram_tensor("mid_x", (32, 128, 512), f32, kind="Internal").ap()
    mid_n = nc.dram_tensor("mid_n", (32, 128, 512), f32, kind="Internal").ap()
    build(nc, *args, mamba_w, out, mid_x, mid_n)
    got = run(nc, [arrays], core_ids=[0]).results[0]["out_0"]
    return np.ascontiguousarray(
        np.asarray(got).reshape(32, 2, 64, 16, 32).transpose(0, 3, 1, 4, 2).reshape(32, 32, 32, 64))
```
